# Optimizing a Trainium2 kernel written in Bass

```python
import numpy as np
import jax
import jax.numpy as jnp

def _softmax(x, axis=-1):
    return jax.nn.softmax(x, axis=axis)

def _gelu(x):
    return jax.nn.gelu(x, approximate=True)

def _silu(x):
    return jax.nn.silu(x)

def _sigmoid(x):
    return jax.nn.sigmoid(x)

def _layernorm(x, axis=-1, eps=1e-05):
    m = jnp.mean(x, axis=axis, keepdims=True)
    v = jnp.var(x, axis=axis, keepdims=True)
    return (x - m) / jnp.sqrt(v + eps)

def _scatter_add(tgt, idx, src, axis=0):
    return tgt.at[idx].add(src)

def _segment_sum(src, seg, n):
    return jax.ops.segment_sum(src, seg, n)
kernel_name = 'mk_adaln_ffn_d1_seqx_r8_1f7107'

def setup_inputs(seed: int=0):
    np.random.seed(seed)
    _w = jnp.asarray

    def _rec_inputs():
        import jax
        import jax.numpy as jnp
        _rk = jax.random.key(seed)
        x = -7.109e-05 + 0.9999 * jax.random.normal(jax.random.fold_in(_rk, 1), (32, 32, 256), jnp.float32)
        _lenS = 32 - jax.random.randint(jax.random.fold_in(_rk, 7), (32,), 0, max(1, 32 // 4) + 1, jnp.int32)
        _lenS2 = 32 - jax.random.randint(jax.random.fold_in(_rk, 8), (32,), 0, max(1, 32 // 4) + 1, jnp.int32)
        itok_B_1_198 = jax.random.randint(jax.random.fold_in(_rk, 11), (32,), 1, 199, jnp.int32)
        return (x, itok_B_1_198)
    x, itok_B_1_198 = _rec_inputs()

    def _L0_cond_setup():
        import jax, jax.numpy as jnp
        import numpy as np
        B, C, T = (128, 32, 256)
        S, D = (200, 32)
        key = jax.random.key(seed)
        k1, k2, k3 = jax.random.split(key, 3)
        x = jax.random.normal(k1, (B, C, T), dtype=jnp.float32)
        conditions = jax.random.randint(k2, (B,), 0, S, dtype=jnp.int64)
        weights = jax.random.normal(k3, (S, C, D), dtype=jnp.float32) / jnp.sqrt(jnp.float32(C))
        return {'x': x, 'conditions': conditions, 'weights': weights}
    _L0_cond_all = _L0_cond_setup()
    _L0_cond_in = {k: v for k, v in _L0_cond_all.items() if k in ('weights',)}
    del _L0_cond_all

    def _L0_ffn_setup():
        import jax, jax.numpy as jnp
        import numpy as np
        from jax import lax
        DIM = 256
        E = 8
        K = 2
        RANK = 32
        CAP_FACTOR = 1.25

        def gelu(x):
            return jax.nn.gelu(x, approximate=False)

        def _moe_forward(x, gate_w, w1, b1, w2, b2, wd, wu, sw1, sb1, sw2, sb2, swd, swu):
            B, S, D = x.shape
            T = B * S
            cap = max(1, int(T * CAP_FACTOR / E))
            xt = x.reshape(T, D)
            logits = xt @ gate_w
            probs_full = jax.nn.softmax(logits, axis=-1)
            top_p, top_i = lax.top_k(probs_full, K)
            out = jnp.zeros_like(xt)
            for k in range(K):
                e = top_i[:, k]
                w = top_p[:, k]
                onehot = jax.nn.one_hot(e, E, dtype=jnp.int32)
                pos_all = jnp.cumsum(onehot, axis=0) - 1
                pos = jnp.take_along_axis(pos_all, e[:, None], axis=1)[:, 0]
                keep = pos < cap
                pos_c = jnp.where(keep, pos, cap)
                buf = jnp.zeros((E, cap, D), x.dtype).at[e, pos_c].set(xt * keep[:, None].astype(x.dtype), mode='drop')
                h = gelu(jnp.einsum('ecd,edf->ecf', buf, w1) + b1[:, None, :])
                y = jnp.einsum('ecf,efd->ecd', h, w2) + b2[:, None, :]
                a = jnp.einsum('ecr,erd->ecd', gelu(jnp.einsum('ecd,edr->ecr', buf, wd)), wu)
                y = y + a
                tok = y[e, jnp.minimum(pos_c, cap - 1)]
                out = out + tok * keep[:, None].astype(x.dtype) * w[:, None]
            sh = gelu(xt @ sw1 + sb1) @ sw2 + sb2
            sh = sh + gelu(xt @ swd) @ swu
            out = out + 0.2 * sh
            return out.reshape(B, S, D)
        key = jax.random.key(seed)
        ks = jax.random.split(key, 16)
        s = 0.02
        d, h = (DIM, 4 * DIM)
        inp = {'x': jax.random.normal(ks[0], (4, 256, d), dtype=jnp.float32), 'gate_w': jax.random.normal(ks[1], (d, E), dtype=jnp.float32) * s, 'w1': jax.random.normal(ks[2], (E, d, h), dtype=jnp.float32) * s, 'b1': jnp.zeros((E, h), dtype=jnp.float32), 'w2': jax.random.normal(ks[3], (E, h, d), dtype=jnp.float32) * s, 'b2': jnp.zeros((E, d), dtype=jnp.float32), 'wd': jax.random.normal(ks[4], (E, d, RANK), dtype=jnp.float32) * s, 'wu': jax.random.normal(ks[5], (E, RANK, d), dtype=jnp.float32) * s, 'sw1': jax.random.normal(ks[6], (d, h), dtype=jnp.float32) * s, 'sb1': jnp.zeros((h,), dtype=jnp.float32), 'sw2': jax.random.normal(ks[7], (h, d), dtype=jnp.float32) * s, 'sb2': jnp.zeros((d,), dtype=jnp.float32), 'swd': jax.random.normal(ks[8], (d, RANK), dtype=jnp.float32) * s, 'swu': jax.random.normal(ks[9], (RANK, d), dtype=jnp.float32) * s}
        return inp
    _L0_ffn_all = _L0_ffn_setup()
    _L0_ffn_in = {k: v for k, v in _L0_ffn_all.items() if k in ('gate_w', 'w1', 'b1', 'w2', 'b2', 'wd', 'wu', 'sw1', 'sb1', 'sw2', 'sb2', 'swd', 'swu')}
    del _L0_ffn_all
    return {'x': x, 'itok_B_1_198': itok_B_1_198, 'L0_cond_weights': _L0_cond_in['weights'], 'L0_ffn_gate_w': _L0_ffn_in['gate_w'], 'L0_ffn_w1': _L0_ffn_in['w1'], 'L0_ffn_b1': _L0_ffn_in['b1'], 'L0_ffn_w2': _L0_ffn_in['w2'], 'L0_ffn_b2': _L0_ffn_in['b2'], 'L0_ffn_wd': _L0_ffn_in['wd'], 'L0_ffn_wu': _L0_ffn_in['wu'], 'L0_ffn_sw1': _L0_ffn_in['sw1'], 'L0_ffn_sb1': _L0_ffn_in['sb1'], 'L0_ffn_sw2': _L0_ffn_in['sw2'], 'L0_ffn_sb2': _L0_ffn_in['sb2'], 'L0_ffn_swd': _L0_ffn_in['swd'], 'L0_ffn_swu': _L0_ffn_in['swu']}

def reference(x, itok_B_1_198, L0_cond_weights, L0_ffn_gate_w, L0_ffn_w1, L0_ffn_b1, L0_ffn_w2, L0_ffn_b2, L0_ffn_wd, L0_ffn_wu, L0_ffn_sw1, L0_ffn_sb1, L0_ffn_sw2, L0_ffn_sb2, L0_ffn_swd, L0_ffn_swu):
    import jax
    import jax.numpy as jnp

    def _L0_cond_ref(x, conditions, weights):
        import jax, jax.numpy as jnp
        import numpy as np
        B, C, T = (128, 32, 256)
        S, D = (200, 32)
        w = weights[conditions]
        return jnp.einsum('bct,bcd->bdt', x, w)

    def _L0_ffn_ref(x, gate_w, w1, b1, w2, b2, wd, wu, sw1, sb1, sw2, sb2, swd, swu):
        import jax, jax.numpy as jnp
        import numpy as np
        from jax import lax
        DIM = 256
        E = 8
        K = 2
        RANK = 32
        CAP_FACTOR = 1.25

        def gelu(x):
            return jax.nn.gelu(x, approximate=False)

        def _moe_forward(x, gate_w, w1, b1, w2, b2, wd, wu, sw1, sb1, sw2, sb2, swd, swu):
            B, S, D = x.shape
            T = B * S
            cap = max(1, int(T * CAP_FACTOR / E))
            xt = x.reshape(T, D)
            logits = xt @ gate_w
            probs_full = jax.nn.softmax(logits, axis=-1)
            top_p, top_i = lax.top_k(probs_full, K)
            out = jnp.zeros_like(xt)
            for k in range(K):
                e = top_i[:, k]
                w = top_p[:, k]
                onehot = jax.nn.one_hot(e, E, dtype=jnp.int32)
                pos_all = jnp.cumsum(onehot, axis=0) - 1
                pos = jnp.take_along_axis(pos_all, e[:, None], axis=1)[:, 0]
                keep = pos < cap
                pos_c = jnp.where(keep, pos, cap)
                buf = jnp.zeros((E, cap, D), x.dtype).at[e, pos_c].set(xt * keep[:, None].astype(x.dtype), mode='drop')
                h = gelu(jnp.einsum('ecd,edf->ecf', buf, w1) + b1[:, None, :])
                y = jnp.einsum('ecf,efd->ecd', h, w2) + b2[:, None, :]
                a = jnp.einsum('ecr,erd->ecd', gelu(jnp.einsum('ecd,edr->ecr', buf, wd)), wu)
                y = y + a
                tok = y[e, jnp.minimum(pos_c, cap - 1)]
                out = out + tok * keep[:, None].astype(x.dtype) * w[:, None]
            sh = gelu(xt @ sw1 + sb1) @ sw2 + sb2
            sh = sh + gelu(xt @ swd) @ swu
            out = out + 0.2 * sh
            return out.reshape(B, S, D)
        return _moe_forward(x, gate_w, w1, b1, w2, b2, wd, wu, sw1, sb1, sw2, sb2, swd, swu)
    x = x + _L0_ffn_ref(_L0_cond_ref(x, itok_B_1_198, L0_cond_weights), L0_ffn_gate_w, L0_ffn_w1, L0_ffn_b1, L0_ffn_w2, L0_ffn_b2, L0_ffn_wd, L0_ffn_wu, L0_ffn_sw1, L0_ffn_sb1, L0_ffn_sw2, L0_ffn_sb2, L0_ffn_swd, L0_ffn_swu)
    return x

_drawn_inputs = setup_inputs


def setup_inputs(seed=0):
    import zlib

    import numpy as np

    out = dict(_drawn_inputs(seed))
    spreads = {'L0_ffn_b1': (0.0, 0.8),
     'L0_ffn_b2': (0.0, 0.318),
     'L0_ffn_sb1': (0.0, 0.8),
     'L0_ffn_sb2': (0.0, 0.374)}
    factors = {'L0_ffn_wd': 8.0, 'L0_ffn_wu': 8.0, 'L0_ffn_swd': 8.0, 'L0_ffn_swu': 8.0}
    for name, (base, spread) in spreads.items():
        noise = np.random.default_rng([zlib.crc32(name.encode()), seed]).standard_normal(out[name].shape)
        drawn = base * np.exp(spread * noise) if base else spread * noise
        out[name] = jnp.asarray(drawn.astype(out[name].dtype))
    for name, factor in factors.items():
        out[name] = (out[name] * factor).astype(out[name].dtype)
    return out
```

```python
from contextlib import ExitStack

import concourse.bass as bass
from concourse import mybir

F32 = mybir.dt.float32
F32R = mybir.dt.float32r
BF16 = mybir.dt.bfloat16
I32 = mybir.dt.int32
U32 = mybir.dt.uint32
ALU = mybir.AluOpType
ACT = mybir.ActivationFunctionType
AX_X = mybir.AxisListType.X

P = 128
B, C, D = 32, 32, 256
T = B * C
NT = T // P
SPT = P // C
E, K = 8, 2
H = 4 * D
RANK = 32
CAP = int(T * 1.25 / E)
SLOTS = K * CAP
SHARED_SCALE = 0.2
KD = D // P
NF = H // P
HT = NF + 1
HALF = T // 2
HTILES = HALF // P
ROW = D + 4
W_COL, ID_COL = D, D + 1
ST = (SLOTS + P - 1) // P
ST_ROWS = [min(P, SLOTS - s * P) for s in range(ST)]
CHUNKS = 4
FC = H // CHUNKS
FT = NF // CHUNKS
SIDE = 4
PAST_END = float(1 << 20)
N_BIAS1, N_SBIAS1 = E * NF, NF
N_BIAS = N_BIAS1 + N_SBIAS1 + E * KD


def build(nc, x, itok, cond_w, gate_w, w1, b1, w2, b2, wd, wu, sw1, sb1, sw2, sb2, swd, swu, out, slot_rows):
    with ExitStack() as ctx:
        def sb(name, shape, dt=F32):
            return ctx.enter_context(nc.sbuf_tensor(name, shape, dt))

        def bank(name):
            return ctx.enter_context(nc.psum_tensor(name, [P, 512], F32))

        def sem(name):
            return ctx.enter_context(nc.semaphore(name))

        hid_ps = [bank(f"hid_ps{i}") for i in range(3)]
        y_ps = [bank(f"y_ps{i}") for i in range(2)]
        turn_ps = [bank(f"turn_ps{i}") for i in range(2)]
        row_ps = bank("row_ps")

        ident = sb("ident", [P, P])
        before = sb("before", [P, P], BF16)
        ones = sb("ones", [P, P], BF16)
        rank_of = sb("rank_of", [P, NT, E])
        slot_base = sb("slot_base", [P, NT, K, E])
        slot_local = sb("slot_local", [P, ST])
        channel = sb("channel", [P, SPT])
        itok_all = sb("itok_all", [P, B], I32)
        cond_row = sb("cond_row", [P, NT], I32)
        logits2 = sb("logits2", [P, NT, 2 * E])
        logits = sb("logits", [P, NT, E])
        expd = sb("expd", [P, NT, E])
        is_top = sb("is_top", [P, NT, E])
        best = sb("best", [P, NT])
        top = sb("top", [P, NT])
        denom = sb("denom", [P, NT])
        chosen = sb("chosen", [P, NT, K, E], BF16)
        picked = sb("picked", [P, NT, K, E])
        base_of = sb("base_of", [P, NT, K])
        pos = sb("pos", [P, NT, K])
        slot_f = sb("slot_f", [P, NT, K])
        slot_i = sb("slot_i", [P, NT, K], I32)
        gate_raw = sb("gate_raw", [P, KD, E])
        gate2 = sb("gate2", [P, KD, 2 * E], F32R)
        bias_rows = sb("bias_rows", [P, P])
        bias_t = sb("bias_t", [P, N_BIAS])
        bias_now = [sb(f"bias_now{i}", [P, NF + KD]) for i in range(2)]
        sb2_all = sb("sb2_all", [P, D])
        sb2_scaled = sb("sb2_scaled", [P, D])
        empty_row = sb("empty_row", [P, ROW])

        x_in = sb("x_in", [P, NT, D])
        cond_g = sb("cond_g", [P, NT, C])
        cond_diag = sb("cond_diag", [P, NT, P])
        token_row = [sb(f"token_row{k}", [P, NT, ROW]) for k in range(K)]
        base = sb("base", [P, NT, D])
        xct_h = sb("xct_h", [P, KD, T], F32R)
        xct_l = sb("xct_l", [P, KD, T], F32R)
        slot_in = [sb(f"slot_in{i}", [P, ST, ROW]) for i in range(2)]
        slot_w = [sb(f"slot_w{i}", [P, ST]) for i in range(2)]
        slot_free = sb("slot_free", [P, ST])
        slot_row = sb("slot_row", [P, ST])
        slot_spare = sb("slot_spare", [P, ST])
        slot_tok = [sb(f"slot_tok{i}", [P, ST], I32) for i in range(2)]
        xs_h = sb("xs_h", [P, KD, SLOTS], F32R)
        xs_l = sb("xs_l", [P, KD, SLOTS], F32R)
        y_t = sb("y_t", [P, KD, SLOTS])
        y_row = sb("y_row", [P, ST, D])

        w1_raw = sb("w1_raw", [P, KD, H])
        wd_raw = sb("wd_raw", [P, KD, RANK])
        w2_raw = sb("w2_raw", [P, NF, D])
        wu_raw = sb("wu_raw", [3 * RANK, D])
        w1_h = [sb(f"w1_h{i}", [P, KD, H], F32R) for i in range(2)]
        w1_l = [sb(f"w1_l{i}", [P, KD, H], F32R) for i in range(2)]
        wd_h = [sb(f"wd_h{i}", [P, KD, 3, RANK], F32R) for i in range(2)]
        wd_l = [sb(f"wd_l{i}", [P, KD, 3, RANK], F32R) for i in range(2)]
        w2_h = [sb(f"w2_h{i}", [P, NF, D], F32R) for i in range(2)]
        w2_l = [sb(f"w2_l{i}", [P, NF, D], F32R) for i in range(2)]
        wu_s = [sb(f"wu_s{i}", [3 * RANK, D], F32R) for i in range(2)]
        gelu_f = sb("gelu_f", [P, 3, HALF])
        hid_h = sb("hid_h", [P, NF, HALF], F32R)
        hid_l = sb("hid_l", [P, NF, HALF], F32R)
        low_s = sb("low_s", [3 * RANK, HALF], F32R)

        itok_in = sem("itok_in")
        x_loaded = sem("x_loaded")
        gate_in = sem("gate_in")
        biases_in = sem("biases_in")
        sb2_in = sem("sb2_in")
        w1_in = sem("w1_in")
        wd_in = sem("wd_in")
        w2_in = sem("w2_in")
        wu_in = sem("wu_in")
        cond_in = sem("cond_in")
        slots_in = [sem(f"slots_in{i}") for i in range(2)]
        filled = sem("filled")
        spare_out = sem("spare_out")
        dispatched = sem("dispatched")
        base_out = sem("base_out")
        combined = sem("combined")
        consts = sem("consts")
        ident_made = sem("ident_made")
        empty_made = sem("empty_made")
        diag_zero = sem("diag_zero")
        index_math = sem("index_math")
        diag_made = sem("diag_made")
        xct_made = sem("xct_made")
        xct_hi = sem("xct_hi")
        xct_lo = sem("xct_lo")
        rows_made = sem("rows_made")
        rows_copied = sem("rows_copied")
        rows_twice = sem("rows_twice")
        gate_hi = sem("gate_hi")
        gate_lo = sem("gate_lo")
        logits_made = sem("logits_made")
        logits_copied = sem("logits_copied")
        bias_turned = sem("bias_turned")
        bias_ready = sem("bias_ready")
        bias_set = sem("bias_set")
        route = sem("route")
        centred = sem("centred")
        expd_made = sem("expd_made")
        chosen_made = sem("chosen_made")
        pos_made = sem("pos_made")
        slots_known = sem("slots_known")
        base_math = sem("base_math")
        w1_hi = sem("w1_hi")
        w1_lo = sem("w1_lo")
        wd_hi = sem("wd_hi")
        wd_lo = sem("wd_lo")
        w2_hi = sem("w2_hi")
        w2_lo = sem("w2_lo")
        wu_hi = sem("wu_hi")
        wu_lo = sem("wu_lo")
        hid_made = sem("hid_made")
        hid_gelu = sem("hid_gelu")
        hid_split = sem("hid_split")
        y_made = sem("y_made")
        base_done = sem("base_done")
        y_biased = sem("y_biased")
        y_turned = sem("y_turned")
        y_weighted = sem("y_weighted")
        slots_turned = sem("slots_turned")
        slots_hi = sem("slots_hi")
        slots_lo = sem("slots_lo")
        slot_math = sem("slot_math")
        slots_sided = sem("slots_sided")

        x_v = x.rearrange("b c f -> (b c) f").rearrange("(t p) f -> p t f", p=P)
        out_v = out[0:T, :].rearrange("(t p) f -> p t f", p=P)
        spare_v = out[T:T + SLOTS, :].rearrange("(p j) f -> p j f", p=64)
        cond_v = cond_w.rearrange("s c d -> (s c) d")
        fill_v = slot_rows.rearrange("(p j) f -> p j f", p=P)
        w1_v = w1.rearrange("e (k p) f -> e p k f", p=P)
        w2_v = w2.rearrange("e (t p) f -> e p t f", p=P)
        wd_v = wd.rearrange("e (k p) r -> e p k r", p=P)
        slots_a = slot_rows.rearrange("(e s) f -> e s f", e=E)[:, 0:2 * P, :].rearrange("e (t p) f -> e p t f", p=P)
        slots_b = slot_rows.rearrange("(e s) f -> e s f", e=E)[:, 2 * P:SLOTS, :]

        def hid_count(u, j):
            return u * HT + (j + 1)

        def hid_before(v):
            return v * HT

        def y_before(v):
            return 2 * HTILES + (v - 2) * KD

        block = ctx.enter_context(nc.Block())

        @block.sync
        def _(sp):
            def load_set(v):
                e = v - 1
                sp.wait_ge(w1_lo, v * CHUNKS)
                sp.dma_start(w1_raw[:, :, :], w1_v[e]).then_inc(w1_in, 16)
                sp.wait_ge(wd_lo, v)
                sp.dma_start(wd_raw[:, :, :], wd_v[e]).then_inc(wd_in, 16)
                sp.wait_ge(w2_lo, v * CHUNKS)
                sp.dma_start(w2_raw[:, :, :], w2_v[e]).then_inc(w2_in, 16)
                sp.wait_ge(wu_lo, v)
                for g in range(3):
                    sp.dma_start(wu_raw[g * RANK:(g + 1) * RANK, :], wu[e]).then_inc(wu_in, 16)

            def load_slots(e, par, first=False):
                if not first:
                    sp.wait_ge(slots_turned, (e - 1) * KD)
                    sp.wait_ge(slots_sided, (e - 1) * KD)
                sp.dma_start(slot_in[par][:, 0:2, :], slots_a[e]).then_inc(slots_in[par], 16)
                sp.dma_start(slot_in[par][0:ST_ROWS[2], 2, :], slots_b[e]).then_inc(slots_in[par], 16)

            sp.dma_start(x_in[:, :, :], x_v).then_inc(x_loaded, 16)
            sp.dma_start(w1_raw[:, :, :], sw1.rearrange("(k p) f -> p k f", p=P)).then_inc(w1_in, 16)
            sp.dma_start(wd_raw[:, :, :], swd.rearrange("(k p) r -> p k r", p=P)).then_inc(wd_in, 16)
            sp.dma_start(w2_raw[:, :, :], sw2.rearrange("(t p) f -> p t f", p=P)).then_inc(w2_in, 16)
            for g in range(3):
                sp.dma_start(wu_raw[g * RANK:(g + 1) * RANK, :], swu).then_inc(wu_in, 16)
            sp.wait_ge(empty_made, 2)
            sp.dma_start(fill_v, empty_row[:, :].unsqueeze(1).to_broadcast([P, E * SLOTS // P, ROW])).then_inc(filled, 16)
            sp.dma_start(spare_v, empty_row[0:64, 0:D].unsqueeze(1).to_broadcast([64, SLOTS // 64, D])).then_inc(spare_out, 16)
            load_set(1)
            sp.wait_ge(dispatched, 16 * NT * K)
            sp.wait_ge(consts, 12)
            load_slots(0, 0, first=True)
            load_slots(1, 1, first=True)
            for h in range(2):
                sp.wait_ge(base_done, (h + 1) * HTILES)
                sp.dma_start(out_v[:, h * HTILES:(h + 1) * HTILES, :],
                             base[:, h * HTILES:(h + 1) * HTILES, :]).then_inc(base_out, 16)
                if h == 0:
                    load_set(2)
            load_set(3)
            with sp.Fori(0, (E - 4) // 2) as pair:
                for d in range(2):
                    load_slots(pair * 2 + (2 + d), d % 2)
                    load_set(pair * 2 + (4 + d))
            load_slots(6, 0)
            load_set(8)
            load_slots(7, 1)
            sp.wait_ge(filled, 16)
            sp.wait_ge(spare_out, 16)
            sp.wait_ge(base_out, 32)
            sp.wait_ge(dispatched, 16 * NT * K)
            sp.wait_ge(combined, 16 * ST * E)

        @block.gpsimd
        def _(pool):
            pool.iota(channel[:, :], pattern=[[-C, SPT]], base=0, channel_multiplier=1,
                      allow_small_or_imprecise_dtypes=True).then_inc(consts, 1)
            pool.memset(empty_row[:, :], 0.0).then_inc(empty_made, 1)
            pool.wait_ge(empty_made, 1)
            pool.memset(empty_row[:, ID_COL:ID_COL + 1], float(T)).then_inc(empty_made, 1)
            pool.wait_ge(index_math, SPT * 1)
            for t in range(NT):
                pool.indirect_dma_start(
                    out=cond_g[:, t, :], out_offset=None, in_=cond_v,
                    in_offset=bass.IndirectOffsetOnAxis(ap=cond_row[:, t:t + 1].bitcast(U32), axis=0),
                ).then_inc(cond_in, 16)
            pool.memset(ident[:, :], 0.0).then_inc(ident_made, 1)
            pool.wait_ge(ident_made, 1)
            pool.affine_select(out=ident[:, :], in_=ident[:, :], compare_op=ALU.not_equal, fill=1.0, base=0,
                               pattern=[[-1, P]], channel_multiplier=1).then_inc(ident_made, 1)
            pool.iota(rank_of[:, :, :], pattern=[[0, NT], [-1, E]], base=E, channel_multiplier=0,
                      allow_small_or_imprecise_dtypes=True).then_inc(consts, 1)
            pool.memset(ones[:, :], 1.0).then_inc(consts, 1)
            pool.wait_ge(consts, 3)
            pool.affine_select(out=before[:, :], in_=ones[:, :], compare_op=ALU.is_gt, fill=0.0, base=0,
                               pattern=[[1, P]], channel_multiplier=-1).then_inc(consts, 1)
            pool.iota(slot_base[:, :, :, :], pattern=[[0, NT], [CAP, K], [SLOTS, E]], base=0, channel_multiplier=0,
                      allow_small_or_imprecise_dtypes=True).then_inc(consts, 1)
            pool.iota(slot_local[:, :], pattern=[[P, ST]], base=0, channel_multiplier=1,
                      allow_small_or_imprecise_dtypes=True).then_inc(consts, 1)
            for k in range(K):
                pool.iota(token_row[k][:, :, ID_COL], pattern=[[P, NT]], base=0, channel_multiplier=1,
                          allow_small_or_imprecise_dtypes=True).then_inc(consts, 1)
                pool.memset(token_row[k][:, :, ID_COL + 1:ROW], 0.0).then_inc(consts, 1)
            for i in range(2):
                pool.memset(slot_in[i][:, ST - 1, D:ROW], 0.0).then_inc(consts, 1)

            def apart(semaphore, count):
                if not isinstance(count, int):
                    count = pool.to_reg(count)
                    pool.wait_ge(ident_made, 2)
                pool.wait_ge(semaphore, count)

            def split_hi(v, par, waits=True):
                if waits:
                    pool.wait_ge(hid_made, hid_before(v))
                apart(wd_in, 16 * (v + 1))
                for g in range(3):
                    ins = pool.tensor_copy(wd_h[par][:, :, g, :], wd_raw[:, :, :])
                ins.then_inc(wd_hi, 1)
                if waits:
                    pool.wait_ge(y_made, y_before(v))
                apart(wu_in, 48 * (v + 1))
                pool.tensor_copy(wu_s[par][:, :], wu_raw[:, :]).then_inc(wu_hi, 1)
                apart(w2_in, 16 * (v + 1))
                for c in range(CHUNKS):
                    pool.tensor_copy(w2_h[par][:, c * FT:(c + 1) * FT, :],
                                     w2_raw[:, c * FT:(c + 1) * FT, :]).then_inc(w2_hi, 1)

            def set_bias(e, par):
                pool.tensor_copy(bias_now[par][:, 0:NF], bias_t[:, bass.ds(e * NF, NF)]).then_inc(bias_set, 1)
                pool.tensor_copy(bias_now[par][:, NF:NF + KD],
                                 bias_t[:, bass.ds(e * KD + (N_BIAS1 + N_SBIAS1), KD)]).then_inc(bias_set, 1)

            def side_data(e, par):
                apart(slots_in[par], (e + (2 - par)) * 16)
                pool.tensor_copy(slot_w[par][:, :], slot_in[par][:, :, W_COL]).then_inc(slot_math, 1)
                pool.tensor_scalar(slot_free[:, :], slot_in[par][:, :, ID_COL], float(T), None,
                                   ALU.is_ge).then_inc(slot_math, 1)
                pool.wait_ge(slot_math, e * SIDE + 2)
                pool.tensor_tensor(slot_spare[:, :], slot_free[:, :], slot_local[:, :], ALU.mult).then_inc(slot_math, 1)
                pool.wait_ge(slot_math, e * SIDE + 3)
                pool.tensor_tensor(slot_row[:, :], slot_spare[:, :], slot_in[par][:, :, ID_COL],
                                   ALU.add).then_inc(slot_math, 1)
                apart(slot_math, e * SIDE + 4)
                pool.tensor_copy(slot_tok[par][:, :], slot_row[:, :]).then_inc(slots_sided, KD)

            def combine(e, par):
                pool.wait_ge(y_weighted, (e + 1) * ST)
                apart(slots_sided, (e + 1) * KD)
                if not isinstance(e, int) or e > 0:
                    apart(combined, e * (16 * ST))
                for s in range(ST):
                    n = ST_ROWS[s]
                    pool.indirect_dma_start(
                        out=out, out_offset=bass.IndirectOffsetOnAxis(ap=slot_tok[par][0:n, s:s + 1].bitcast(U32), axis=0),
                        in_=y_row[0:n, s, :], in_offset=None, bounds_check=T + SLOTS - 1,
                        compute_op=ALU.add).then_inc(combined, 16)

            split_hi(0, 0, waits=False)
            for t in range(NT):
                pool.wait_ge(rows_copied, t + 1)
                pool.tensor_copy(token_row[1][:, t, 0:D], token_row[0][:, t, 0:D]).then_inc(rows_twice, 1)
            pool.wait_ge(rows_twice, NT)
            pool.wait_ge(slots_known, 3)
            pool.wait_ge(filled, 16)
            for t in range(NT):
                for k in range(K):
                    pool.indirect_dma_start(
                        out=slot_rows, out_offset=bass.IndirectOffsetOnAxis(ap=slot_i[:, t, k:k + 1].bitcast(U32), axis=0),
                        in_=token_row[k][:, t, :], in_offset=None, bounds_check=E * SLOTS - 1,
                        oob_is_err=False).then_inc(dispatched, 16)
            pool.wait_ge(sb2_in, 16)
            pool.tensor_scalar(sb2_scaled[:, :], sb2_all[:, :], SHARED_SCALE, None, ALU.mult).then_inc(base_math, 1)
            pool.wait_ge(base_math, 1)
            pool.wait_ge(x_loaded, 16)
            for t in range(NT):
                pool.tensor_tensor(base[:, t, :], x_in[:, t, :], sb2_scaled[:, :], ALU.add).then_inc(base_math, 1)
            pool.wait_ge(bias_ready, 1)
            set_bias(0, 0)
            split_hi(1, 1, waits=False)

            def period(e, par, combine_one=True, split=True, biases=True):
                if split:
                    split_hi(e + 2, par)
                if combine_one:
                    combine(e - 1, 1 - par)
                side_data(e, par)
                if biases:
                    if combine_one:
                        apart(y_biased, e * KD)
                    set_bias(e + 1, 1 - par)

            period(0, 0, combine_one=False)
            pool.wait_ge(base_out, 32)
            pool.wait_ge(spare_out, 16)
            with pool.Fori(0, (E - 2) // 2) as pair:
                for d in range(2):
                    period(pair * 2 + (1 + d), (1 + d) % 2)
            period(7, 1, split=False, biases=False)
            combine(7, 1)

        @block.scalar
        def _(act):
            act.dma_start(itok_all[:, :], itok.partition_broadcast(P)).then_inc(itok_in, 16)
            act.dma_start(gate_raw[:, :, :], gate_w.rearrange("(k p) e -> p k e", p=P)).then_inc(gate_in, 16)
            act.dma_start(bias_rows[0:N_BIAS1, :], b1.rearrange("e (t p) -> (e t) p", p=P)).then_inc(biases_in, 16)
            act.dma_start(bias_rows[N_BIAS1:N_BIAS1 + N_SBIAS1, :],
                          sb1.rearrange("(t p) -> t p", p=P)).then_inc(biases_in, 16)
            act.dma_start(bias_rows[N_BIAS1 + N_SBIAS1:N_BIAS, :],
                          b2.rearrange("e (t p) -> (e t) p", p=P)).then_inc(biases_in, 16)
            act.dma_start(sb2_all[:, :], sb2.partition_broadcast(P)).then_inc(sb2_in, 16)

            def w1_chunk(v, par, c):
                if c == 0:
                    act.wait_ge(w1_in, 16 * (v + 1))
                act.activation(w1_h[par][:, :, c * FC:(c + 1) * FC], w1_raw[:, :, c * FC:(c + 1) * FC],
                               ACT.Copy).then_inc(w1_hi, 1)

            act.wait_ge(gate_in, 16)
            act.activation(gate2[:, :, 0:E], gate_raw[:, :, :], ACT.Copy).then_inc(gate_hi, 1)
            w1_chunk(0, 0, 0)
            w1_chunk(0, 0, 1)
            act.wait_ge(bias_turned, 1)
            act.activation(bias_t[:, :], row_ps[:, 0:N_BIAS], ACT.Copy).then_inc(bias_ready, 1)
            for h in range(2):
                for k in range(KD):
                    act.wait_ge(xct_made, h * KD + k + 1)
                    src = hid_ps[k] if h == 0 else turn_ps[k]
                    act.activation(xct_h[:, k, h * HALF:(h + 1) * HALF], src[:, :], ACT.Copy).then_inc(xct_hi, 1)
            w1_chunk(0, 0, 2)
            w1_chunk(0, 0, 3)
            row_banks = [y_ps[0], y_ps[1], row_ps, hid_ps[2]]
            for t in range(NT):
                act.wait_ge(rows_made, 2 * (t // 2) + 2)
                act.activation(token_row[0][:, t, 0:D], row_banks[t // 2][:, (t % 2) * D:(t % 2 + 1) * D],
                               ACT.Copy).then_inc(rows_copied, 1)
            act.wait_ge(logits_made, 1)
            act.activation(logits2[:, :, :], turn_ps[0][:, 0:NT * 2 * E].rearrange("p (t e) -> p t e", t=NT),
                           ACT.Copy).then_inc(logits_copied, 1)
            act.wait_ge(centred, 1)
            act.activation(expd[:, :, :], logits[:, :, :], ACT.Exp).then_inc(expd_made, 1)

            def gelu_tile(u, j, n, bias):
                act.wait_ge(hid_made, hid_count(u, j))
                if isinstance(u, int) and u == 0 and j < 3:
                    pass
                else:
                    act.wait_ge(hid_split, hid_count(u, j) - 3)
                src = hid_ps[j % 3]
                if j == 0:
                    act.activation(gelu_f[2 * RANK:3 * RANK, 0, 0:n], src[2 * RANK:3 * RANK, 0:n], ACT.Gelu)
                    act.activation(low_s[:, 0:n], src[0:3 * RANK, 0:n], ACT.Gelu).then_inc(hid_gelu, 1)
                else:
                    act.activation(gelu_f[:, j % 3, 0:n], src[:, 0:n], ACT.Gelu, bias=bias(j - 1))
                    act.activation(hid_h[:, j - 1, 0:n], src[:, 0:n], ACT.Gelu, bias=bias(j - 1)).then_inc(hid_gelu, 1)

            def slots_hi_part():
                for k in range(KD):
                    act.activation(xs_h[:, k, :], turn_ps[k][:, 0:SLOTS], ACT.Copy).then_inc(slots_hi, 1)

            shared_bias = lambda f: bias_t[:, N_BIAS1 + f:N_BIAS1 + f + 1]
            for j in range(HT):
                gelu_tile(0, j, HALF, shared_bias)
            for j in range(HT):
                gelu_tile(1, j, HALF, shared_bias)
                if j < CHUNKS:
                    w1_chunk(1, 1, j)
            act.wait_ge(slots_turned, KD)
            slots_hi_part()

            def period(e, par, split=True):
                act.wait_ge(bias_set, e * 2 + 2)
                for j in range(HT):
                    gelu_tile(e + 2, j, SLOTS, lambda f: bias_now[par][:, f:f + 1])
                    if split and j < CHUNKS:
                        w1_chunk(e + 2, par, j)
                if split:
                    act.wait_ge(slots_turned, e * KD + 2 * KD)
                    slots_hi_part()
                for m in range(KD):
                    act.wait_ge(y_made, 2 * HTILES + (e * KD + (m + 1)))
                    act.activation(y_t[:, m, :], y_ps[m][:, 0:SLOTS], ACT.Identity,
                                   bias=bias_now[par][:, NF + m:NF + m + 1]).then_inc(y_biased, 1)

            period(0, 0)
            with act.Fori(0, (E - 2) // 2) as pair:
                for d in range(2):
                    period(pair * 2 + (1 + d), (1 + d) % 2)
            period(7, 1, split=False)

        @block.vector
        def _(dve):
            dve.memset(cond_diag[:, :, :], 0.0).then_inc(diag_zero, 1)
            dve.wait_ge(itok_in, 16)
            dve.wait_ge(consts, 1)
            itok_v = itok_all[:, :].rearrange("p (t g) -> p t g", g=SPT)
            for g in range(SPT):
                rows = slice(g * C, (g + 1) * C)
                dve.tensor_scalar(cond_row[rows, :], itok_v[rows, :, g], float(C), channel[rows, g:g + 1],
                                  ALU.mult, ALU.add).then_inc(index_math, 1)
            dve.wait_ge(gate_in, 16)
            dve.wait_ge(gate_hi, 1)
            dve.tensor_tensor(gate2[:, :, E:2 * E], gate_raw[:, :, :], gate2[:, :, 0:E].bitcast(F32),
                              ALU.subtract).then_inc(gate_lo, 1)

            def w1_chunk(c, par, v):
                dve.wait_ge(w1_hi, v * CHUNKS + (c + 1))
                cols = slice(c * FC, (c + 1) * FC)
                dve.tensor_tensor(w1_l[par][:, :, cols], w1_raw[:, :, cols], w1_h[par][:, :, cols].bitcast(F32),
                                  ALU.subtract).then_inc(w1_lo, 1)

            def w2_chunk(c, par, v):
                dve.wait_ge(w2_hi, v * CHUNKS + (c + 1))
                rows = slice(c * FT, (c + 1) * FT)
                dve.tensor_tensor(w2_l[par][:, rows, :], w2_raw[:, rows, :], w2_h[par][:, rows, :].bitcast(F32),
                                  ALU.subtract).then_inc(w2_lo, 1)

            def small_chunks(par, v):
                dve.wait_ge(wd_hi, v + 1)
                for g in range(3):
                    ins = dve.tensor_tensor(wd_l[par][:, :, g, :], wd_raw[:, :, :], wd_h[par][:, :, g, :].bitcast(F32),
                                            ALU.subtract)
                ins.then_inc(wd_lo, 1)
                dve.wait_ge(wu_hi, v + 1)
                mid = slice(RANK, 2 * RANK)
                dve.tensor_tensor(wu_s[par][mid, :], wu_raw[mid, :], wu_s[par][mid, :].bitcast(F32),
                                  ALU.subtract).then_inc(wu_lo, 1)

            def split_tile(u, j, n):
                dve.wait_ge(hid_gelu, hid_count(u, j))
                if j == 0:
                    lo = slice(2 * RANK, 3 * RANK)
                    dve.tensor_tensor(low_s[lo, 0:n], gelu_f[lo, 0, 0:n], low_s[lo, 0:n].bitcast(F32),
                                      ALU.subtract).then_inc(hid_split, 1)
                else:
                    dve.tensor_tensor(hid_l[:, j - 1, 0:n], gelu_f[:, j % 3, 0:n], hid_h[:, j - 1, 0:n].bitcast(F32),
                                      ALU.subtract).then_inc(hid_split, 1)

            w1_chunk(0, 0, 0)
            dve.wait_ge(cond_in, 16 * NT)
            dve.wait_ge(diag_zero, 1)
            for g in range(SPT):
                rows = slice(g * C, (g + 1) * C)
                dve.tensor_copy(cond_diag[rows, :, rows], cond_g[rows, :, :]).then_inc(diag_made, 1)
            w1_chunk(1, 0, 0)
            small_chunks(0, 0)
            for h in range(2):
                for k in range(KD):
                    dve.wait_ge(xct_hi, h * KD + k + 1)
                    src = hid_ps[k] if h == 0 else turn_ps[k]
                    cols = slice(h * HALF, (h + 1) * HALF)
                    dve.tensor_tensor(xct_l[:, k, cols], src[:, :], xct_h[:, k, cols].bitcast(F32),
                                      ALU.subtract).then_inc(xct_lo, 1)
            w1_chunk(2, 0, 0)
            w1_chunk(3, 0, 0)

            steps = [0]

            def step(ins):
                steps[0] += 1
                ins.then_inc(route, 1)
                dve.wait_ge(route, steps[0])

            def over_e(ap):
                return ap.unsqueeze(2).to_broadcast([P, NT, E])

            dve.wait_ge(logits_copied, 1)
            step(dve.tensor_tensor(logits[:, :, :], logits2[:, :, 0:E], logits2[:, :, E:2 * E], ALU.add))
            step(dve.tensor_reduce(top[:, :], logits[:, :, :], AX_X, ALU.max))
            dve.tensor_tensor(logits[:, :, :], logits[:, :, :], over_e(top[:, :]), ALU.subtract).then_inc(centred, 1)
            dve.wait_ge(expd_made, 1)
            step(dve.tensor_reduce(denom[:, :], expd[:, :, :], AX_X, ALU.add))
            step(dve.reciprocal(denom[:, :], denom[:, :]))
            dve.wait_ge(consts, 12)
            for k in range(K):
                step(dve.tensor_reduce(top[:, :], expd[:, :, :], AX_X, ALU.max))
                step(dve.tensor_tensor(is_top[:, :, :], expd[:, :, :], over_e(top[:, :]), ALU.is_equal))
                step(dve.tensor_tensor(is_top[:, :, :], is_top[:, :, :], rank_of[:, :, :], ALU.mult))
                step(dve.tensor_reduce(best[:, :], is_top[:, :, :], AX_X, ALU.max))
                step(dve.tensor_tensor(chosen[:, :, k, :], rank_of[:, :, :], over_e(best[:, :]), ALU.is_equal))
                if k == 0:
                    step(dve.scalar_tensor_tensor(out=expd[:, :, :], in0=chosen[:, :, k, :], scalar=-4.0,
                                                  in1=expd[:, :, :], op0=ALU.mult, op1=ALU.add))
                step(dve.tensor_tensor(token_row[k][:, :, W_COL], top[:, :], denom[:, :], ALU.mult))
            dve.engine_nop().then_inc(chosen_made, 1)
            step(dve.tensor_tensor(picked[:, :, :, :], chosen[:, :, :, :], slot_base[:, :, :, :], ALU.mult))
            step(dve.tensor_reduce(base_of[:, :, :], picked[:, :, :, :], AX_X, ALU.add))

            def place_tokens():
                dve.wait_ge(pos_made, 1)
                step(dve.tensor_tensor(picked[:, :, :, :],
                                       turn_ps[0][:, 0:NT * K * E].rearrange("p (t k e) -> p t k e", t=NT, k=K),
                                       chosen[:, :, :, :], ALU.mult))
                step(dve.tensor_reduce(pos[:, :, :], picked[:, :, :, :], AX_X, ALU.add))
                dve.tensor_scalar(slot_f[:, :, :], pos[:, :, :], float(CAP), PAST_END, ALU.is_ge,
                                  ALU.mult).then_inc(slots_known, 1)
                step(dve.tensor_tensor(base_of[:, :, :], base_of[:, :, :], pos[:, :, :], ALU.add))
                dve.wait_ge(slots_known, 1)
                dve.tensor_tensor(slot_i[:, :, :], base_of[:, :, :], slot_f[:, :, :], ALU.add).then_inc(slots_known, 2)

            def shared_rows(h):
                for t in range(h * HTILES, (h + 1) * HTILES):
                    dve.wait_ge(y_made, t + 1)
                    dve.scalar_tensor_tensor(out=base[:, t, :], in0=y_ps[t % 2][:, 0:D], scalar=SHARED_SCALE,
                                             in1=base[:, t, :], op0=ALU.mult, op1=ALU.add).then_inc(base_done, 1)

            def slots_lo_part(e):
                for k in range(KD):
                    dve.wait_ge(slots_hi, e * KD + (k + 1))
                    dve.tensor_tensor(xs_l[:, k, :], turn_ps[k][:, 0:SLOTS], xs_h[:, k, :].bitcast(F32),
                                      ALU.subtract).then_inc(slots_lo, 1)

            def weigh_rows(e, par):
                if not isinstance(e, int) or e > 0:
                    dve.wait_ge(combined, e * (16 * ST))
                dve.wait_ge(slot_math, e * SIDE + 1)
                for s in range(ST):
                    n = ST_ROWS[s]
                    dve.wait_ge(y_turned, e * ST + max(2, s + 1))
                    src = row_ps[0:n, s * D:(s + 1) * D] if s < 2 else y_ps[0][0:n, 0:D]
                    dve.tensor_scalar(y_row[0:n, s, :], src, slot_w[par][0:n, s:s + 1], None,
                                      ALU.mult).then_inc(y_weighted, 1)

            for j in range(HT):
                split_tile(0, j, HALF)
                if j < CHUNKS:
                    w2_chunk(j, 0, 0)
                if j == 4:
                    place_tokens()
            dve.wait_ge(base_math, NT + 1)
            shared_rows(0)
            for j in range(HT):
                split_tile(1, j, HALF)
                if j < CHUNKS:
                    w1_chunk(j, 1, 1)
                elif j < 2 * CHUNKS:
                    w2_chunk(j - CHUNKS, 1, 1)
            small_chunks(1, 1)
            shared_rows(1)
            slots_lo_part(0)

            def period(e, par, rows=True, split=True):
                for j in range(HT):
                    split_tile(e + 2, j, SLOTS)
                    if split and j < CHUNKS:
                        w1_chunk(j, par, e + 2)
                    elif split and j < 2 * CHUNKS:
                        w2_chunk(j - CHUNKS, par, e + 2)
                    if rows and j == 3:
                        weigh_rows(e - 1, 1 - par)
                if split:
                    small_chunks(par, e + 2)
                    slots_lo_part(e + 1)

            period(0, 0, rows=False)
            with dve.Fori(0, (E - 2) // 2) as pair:
                for d in range(2):
                    period(pair * 2 + (1 + d), (1 + d) % 2)
            period(7, 1, split=False)
            weigh_rows(7, 1)

        @block.tensor
        def _(pe):
            def three(out_ap, l_h, l_l, r_h, r_l, start, stop):
                pe.matmul(out_ap, l_h, r_h, start=start, stop=False)
                pe.matmul(out_ap, l_h, r_l, start=False, stop=False)
                return pe.matmul(out_ap, l_l, r_h, start=False, stop=stop)

            pe.wait_ge(ident_made, 2)
            pe.wait_ge(biases_in, 48)
            pe.transpose(row_ps[:, 0:N_BIAS], bias_rows[0:N_BIAS, :], ident[0:N_BIAS, 0:N_BIAS]).then_inc(bias_turned, 1)
            pe.wait_ge(x_loaded, 16)
            pe.wait_ge(diag_made, SPT)
            for h in range(2):
                for k in range(KD):
                    dst = hid_ps[k] if h == 0 else turn_ps[k]
                    for t in range(HTILES):
                        ins = pe.matmul(dst[:, t * P:(t + 1) * P], x_in[:, h * HTILES + t, k * P:(k + 1) * P],
                                        cond_diag[:, h * HTILES + t, :], start=True, stop=True)
                    ins.then_inc(xct_made, 1)
            pe.wait_ge(bias_ready, 1)
            row_banks = [y_ps[0], y_ps[1], row_ps, hid_ps[2]]
            for t in range(NT):
                pe.matmul(row_banks[t // 2][:, (t % 2) * D:(t % 2 + 1) * D], cond_diag[:, t, :], x_in[:, t, :],
                          start=True, stop=True).then_inc(rows_made, 1)
            pe.wait_ge(gate_lo, 1)
            pe.wait_ge(xct_lo, 2 * KD)
            for t in range(NT):
                cols = slice(t * P, (t + 1) * P)
                for k in range(KD):
                    dst = turn_ps[0][:, t * 2 * E:(t + 1) * 2 * E]
                    pe.matmul(dst, xct_h[:, k, cols], gate2[:, k, :], start=(k == 0), stop=False)
                    ins = pe.matmul(dst, xct_l[:, k, cols], gate2[:, k, :], start=False, stop=(k == KD - 1))
            ins.then_inc(logits_made, 1)

            def count_before():
                pe.wait_ge(chosen_made, 1)
                flat = chosen[:, :, :, :].rearrange("p t k e -> p (t k e)")
                w = K * E
                for s in range(NT - 1, 0, -1):
                    pe.matmul(turn_ps[0][:, s * w:NT * w], ones[:, :], flat[:, 0:(NT - s) * w], start=(s == NT - 1),
                              stop=False, skip_group_check=True)
                ins = pe.matmul(turn_ps[0][:, 0:NT * w], before[:, :], flat, start=False, stop=True,
                                skip_group_check=True)
                ins.then_inc(pos_made, 1)

            def hidden(u, j, par, v, x_h, x_l, cols, n):
                if j > 0 and (j - 1) % FT == 0:
                    pe.wait_ge(w1_lo, v * CHUNKS + ((j - 1) // FT + 1))
                if j == 0:
                    pe.wait_ge(wd_lo, v + 1)
                if not isinstance(u, int) or u > 0 or j >= 3:
                    pe.wait_ge(hid_gelu, hid_count(u, j) - 3)
                m = 3 * RANK if j == 0 else P
                dst = hid_ps[j % 3][0:m, 0:n]
                for k in range(KD):
                    if j == 0:
                        l_h, l_l = (w[:, k, :, :].rearrange("p g r -> p (g r)") for w in (wd_h[par], wd_l[par]))
                    else:
                        l_h, l_l = (w[:, k, (j - 1) * P:j * P] for w in (w1_h[par], w1_l[par]))
                    ins = three(dst, l_h, l_l, x_h[:, k, cols], x_l[:, k, cols], k == 0, k == KD - 1)
                ins.then_inc(hid_made, 1)

            def shared_out(h, t):
                n = h * HTILES + t
                if t == 0:
                    pe.wait_ge(w2_lo, CHUNKS)
                    pe.wait_ge(wu_lo, 1)
                    pe.wait_ge(hid_split, h * HT + HT)
                if n >= 2:
                    pe.wait_ge(base_done, n - 1)
                else:
                    pe.wait_ge(rows_copied, 4)
                dst = y_ps[n % 2][:, 0:D]
                cols = slice(t * P, (t + 1) * P)
                pe.matmul(dst, low_s[:, cols], wu_s[0][:, :], start=True, stop=False)
                for f in range(NF):
                    ins = three(dst, hid_h[:, f, cols], hid_l[:, f, cols], w2_h[0][:, f, :], w2_l[0][:, f, :],
                                False, f == NF - 1)
                ins.then_inc(y_made, 1)

            def expert_out(e, m, par):
                v = e + 1
                if m == 0:
                    pe.wait_ge(w2_lo, v * CHUNKS + CHUNKS)
                    pe.wait_ge(wu_lo, v + 1)
                    if isinstance(e, int) and e == 0:
                        pe.wait_ge(base_done, 2 * HTILES)
                    else:
                        pe.wait_ge(y_weighted, e * ST)
                dst = y_ps[m][:, 0:SLOTS]
                cols = slice(m * P, (m + 1) * P)
                pe.wait_ge(hid_split, hid_count(e + 2, 0))
                pe.matmul(dst, wu_s[par][:, cols], low_s[:, 0:SLOTS], start=True, stop=False)
                for f in range(NF):
                    if m == 0:
                        pe.wait_ge(hid_split, hid_count(e + 2, f + 1))
                    ins = three(dst, w2_h[par][:, f, cols], w2_l[par][:, f, cols], hid_h[:, f, 0:SLOTS],
                                hid_l[:, f, 0:SLOTS], False, f == NF - 1)
                ins.then_inc(y_made, 1)

            def turn_slots(e, par):
                pe.wait_ge(slots_in[par], (e + (2 - par)) * 16)
                if isinstance(e, int) and e == 0:
                    pe.wait_ge(slots_known, 3)
                else:
                    pe.wait_ge(slots_lo, e * KD)
                for k in range(KD):
                    for s in range(ST):
                        n = ST_ROWS[s]
                        ins = pe.transpose(turn_ps[k][:, s * P:s * P + n], slot_in[par][0:n, s, k * P:(k + 1) * P],
                                           ident[0:n, 0:n])
                    ins.then_inc(slots_turned, 1)

            def turn_results(e):
                pe.wait_ge(y_biased, e * KD + KD)
                if not isinstance(e, int) or e > 0:
                    pe.wait_ge(y_weighted, e * ST)
                for s in range(ST):
                    n = ST_ROWS[s]
                    for m in range(KD):
                        dst = (row_ps[0:n, s * D + m * P:s * D + (m + 1) * P] if s < 2
                               else y_ps[0][0:n, m * P:(m + 1) * P])
                        ins = pe.transpose(dst, y_t[:, m, s * P:s * P + n], ident[:, :])
                    ins.then_inc(y_turned, 1)

            for h in range(2):
                cols = slice(h * HALF, (h + 1) * HALF)
                for j in range(HT):
                    if h == 0 and j == 2:
                        pe.wait_ge(rows_copied, NT)
                    hidden(h, j, 0, 0, xct_h, xct_l, cols, HALF)
                    if h == 0 and j == 4:
                        count_before()
                for t in range(HTILES):
                    shared_out(h, t)
                    if h == 1 and t == 1:
                        turn_slots(0, 0)

            def period(e, par, rows=True, nxt=True):
                other = 1 - par
                pe.wait_ge(slots_lo, (e + 1) * KD)
                for j in range(HT):
                    hidden(e + 2, j, other, e + 1, xs_h, xs_l, slice(0, SLOTS), SLOTS)
                    if rows and j == 2:
                        turn_results(e - 1)
                expert_out(e, 0, other)
                if nxt:
                    turn_slots(e + 1, other)
                expert_out(e, 1, other)

            period(0, 0, rows=False)
            with pe.Fori(0, (E - 2) // 2) as pair:
                for d in range(2):
                    period(pair * 2 + (1 + d), (1 + d) % 2)
            period(7, 1, nxt=False)
            turn_results(7)


_INS = ["x", "itok_B_1_198", "L0_cond_weights", "L0_ffn_gate_w", "L0_ffn_w1", "L0_ffn_b1", "L0_ffn_w2", "L0_ffn_b2",
        "L0_ffn_wd", "L0_ffn_wu", "L0_ffn_sw1", "L0_ffn_sb1", "L0_ffn_sw2", "L0_ffn_sb2", "L0_ffn_swd", "L0_ffn_swu"]


def kernel(**inputs):
    import numpy as np
    import concourse.bacc as bacc
    from concourse.bass_utils import run_bass_kernel_spmd

    nc = bacc.Bacc("TRN2", target_bir_lowering=False, num_devices=1)
    arrays, args = {}, []
    for name in _INS:
        a = np.ascontiguousarray(inputs[name])
        arrays[f"in_{name}"] = a
        args.append(nc.dram_tensor(f"in_{name}", a.shape, mybir.dt.from_np(a.dtype), kind="ExternalInput").ap())
    out = nc.dram_tensor("out_rows", (T + SLOTS, D), F32, kind="ExternalOutput").ap()
    slot_rows = nc.dram_tensor("slot_rows", (E * SLOTS, ROW), F32, kind="Internal").ap()
    build(nc, *args, out, slot_rows)
    r = run_bass_kernel_spmd(nc, [arrays], core_ids=[0])
    return r.results[0]["out_rows"][0:T].reshape(B, C, D)
```

```python
from contextlib import ExitStack

import concourse.bass as bass
from concourse import mybir

F32 = mybir.dt.float32
F32R = mybir.dt.float32r
BF16 = mybir.dt.bfloat16
I32 = mybir.dt.int32
U32 = mybir.dt.uint32
ALU = mybir.AluOpType
ACT = mybir.ActivationFunctionType
AX_X = mybir.AxisListType.X

P = 128
B, C, D = 32, 32, 256
T = B * C
NT = T // P
SPT = P // C
E, K = 8, 2
H = 4 * D
RANK = 32
CAP = int(T * 1.25 / E)
SLOTS = K * CAP
SHARED_SCALE = 0.2
KD = D // P
NF = H // P
HT = NF + 1
HALF = T // 2
HTILES = HALF // P
ROW = D + 4
W_COL, ID_COL = D, D + 1
ST = (SLOTS + P - 1) // P
ST_ROWS = [min(P, SLOTS - s * P) for s in range(ST)]
CHUNKS = 4
ACT_W2 = 1
FC = H // CHUNKS
FT = NF // CHUNKS
WARM_UP = 9
SIDE = 4
PAST_END = float(1 << 20)
N_BIAS1, N_SBIAS1 = E * NF, NF
N_BIAS = N_BIAS1 + N_SBIAS1 + E * KD


def build(nc, x, itok, cond_w, gate_w, w1, b1, w2, b2, wd, wu, sw1, sb1, sw2, sb2, swd, swu, out, slot_rows, cond_rows):
    with ExitStack() as ctx:
        def sb(name, shape, dt=F32):
            return ctx.enter_context(nc.sbuf_tensor(name, shape, dt))

        def bank(name):
            return ctx.enter_context(nc.psum_tensor(name, [P, 512], F32))

        def sem(name):
            return ctx.enter_context(nc.semaphore(name))

        hid_ps = [bank(f"hid_ps{i}") for i in range(3)]
        y_ps = [bank(f"y_ps{i}") for i in range(2)]
        turn_ps = [bank(f"turn_ps{i}") for i in range(2)]
        row_ps = bank("row_ps")

        ident = sb("ident", [P, P])
        before = sb("before", [P, P], BF16)
        ones = sb("ones", [P, P], BF16)
        rank_of = sb("rank_of", [P, NT, E])
        slot_base = sb("slot_base", [P, NT, K, E])
        slot_local = sb("slot_local", [P, ST])
        itok_col = sb("itok_col", [B, 1], I32)
        logits2 = sb("logits2", [P, NT, 2 * E])
        logits = sb("logits", [P, NT, E])
        expd = sb("expd", [P, NT, E])
        is_top = sb("is_top", [P, NT, E])
        best = sb("best", [P, NT])
        top = sb("top", [P, NT])
        denom = sb("denom", [P, NT])
        chosen = sb("chosen", [P, NT, K, E], BF16)
        picked = sb("picked", [P, NT, K, E])
        base_of = sb("base_of", [P, NT, K])
        pos = sb("pos", [P, NT, K])
        slot_f = sb("slot_f", [P, NT, K])
        slot_i = sb("slot_i", [P, NT, K], I32)
        gate_raw = sb("gate_raw", [P, KD, E])
        gate2 = sb("gate2", [P, KD, 2 * E], F32R)
        bias_rows = sb("bias_rows", [P, P])
        bias_t = sb("bias_t", [P, N_BIAS])
        bias_now = [sb(f"bias_now{i}", [P, NF + KD]) for i in range(2)]
        sb2_all = sb("sb2_all", [P, D])
        sb2_scaled = sb("sb2_scaled", [P, D])
        empty_row = sb("empty_row", [P, ROW])

        x_in = sb("x_in", [P, NT, D])
        cond_g = sb("cond_g", [B, C * C])
        cond_diag = sb("cond_diag", [P, NT, P])
        token_row = [sb(f"token_row{k}", [P, NT, ROW]) for k in range(K)]
        base = sb("base", [P, NT, D])
        xct_f = base[:, :, :].rearrange("p (k a) f -> p k (a f)", k=KD)
        xct_h = sb("xct_h", [P, KD, T], F32R)
        xct_l = sb("xct_l", [P, KD, T], F32R)
        slot_in = [sb(f"slot_in{i}", [P, ST, ROW]) for i in range(2)]
        slot_w = [sb(f"slot_w{i}", [P, ST]) for i in range(2)]
        slot_free = sb("slot_free", [P, ST])
        slot_row = sb("slot_row", [P, ST])
        slot_spare = sb("slot_spare", [P, ST])
        slot_tok = [sb(f"slot_tok{i}", [P, ST], I32) for i in range(2)]
        xs_h = sb("xs_h", [P, KD, SLOTS], F32R)
        xs_l = sb("xs_l", [P, KD, SLOTS], F32R)
        y_t = sb("y_t", [P, KD, SLOTS])
        y_row = sb("y_row", [P, ST, D])

        w1_raw = sb("w1_raw", [P, KD, H])
        wd_raw = sb("wd_raw", [P, KD, RANK])
        w2_raw = sb("w2_raw", [P, NF, D])
        wu_raw = sb("wu_raw", [3 * RANK, D])
        w1_h = [sb(f"w1_h{i}", [P, KD, H], F32R) for i in range(2)]
        w1_l = [sb(f"w1_l{i}", [P, KD, H], F32R) for i in range(2)]
        wd_h = [sb(f"wd_h{i}", [P, KD, 3, RANK], F32R) for i in range(2)]
        wd_l = [sb(f"wd_l{i}", [P, KD, 3, RANK], F32R) for i in range(2)]
        w2_h = [sb(f"w2_h{i}", [P, NF, D], F32R) for i in range(2)]
        w2_l = [sb(f"w2_l{i}", [P, NF, D], F32R) for i in range(2)]
        wu_s = [sb(f"wu_s{i}", [3 * RANK, D], F32R) for i in range(2)]
        gelu_f = sb("gelu_f", [P, 3, HALF])
        hid_h = sb("hid_h", [P, NF, HALF], F32R)
        hid_l = sb("hid_l", [P, NF, HALF], F32R)
        low_s = sb("low_s", [3 * RANK, HALF], F32R)

        itok_in = sem("itok_in")
        x_loaded = [sem(f"x_loaded{h}") for h in range(2)]
        gate_in = sem("gate_in")
        biases_in = sem("biases_in")
        sb2_in = sem("sb2_in")
        w1_in = sem("w1_in")
        wd_in = sem("wd_in")
        w2_in = sem("w2_in")
        wu_in = sem("wu_in")
        cond_in = sem("cond_in")
        cond_out = sem("cond_out")
        diag_in = sem("diag_in")
        slots_in = [sem(f"slots_in{i}") for i in range(2)]
        filled = sem("filled")
        spare_out = sem("spare_out")
        dispatched = sem("dispatched")
        base_out = sem("base_out")
        combined = sem("combined")
        consts = sem("consts")
        ident_made = sem("ident_made")
        empty_made = sem("empty_made")
        diag_zero = sem("diag_zero")
        xct_made = sem("xct_made")
        xct_hi = sem("xct_hi")
        xct_kept = sem("xct_kept")
        xct_lo = sem("xct_lo")
        rows_made = sem("rows_made")
        rows_copied = sem("rows_copied")
        rows_twice = sem("rows_twice")
        base_made = sem("base_made")
        sb2_made = sem("sb2_made")
        gate_hi = sem("gate_hi")
        gate_lo = sem("gate_lo")
        logits_made = sem("logits_made")
        logits_copied = sem("logits_copied")
        bias_turned = sem("bias_turned")
        bias_ready = sem("bias_ready")
        bias_set = sem("bias_set")
        route = sem("route")
        centred = sem("centred")
        expd_made = sem("expd_made")
        chosen_made = sem("chosen_made")
        pos_made = sem("pos_made")
        slots_known = sem("slots_known")
        w1_hi = sem("w1_hi")
        w1_lo = sem("w1_lo")
        wd_hi = sem("wd_hi")
        wd_lo = sem("wd_lo")
        w2_hi = [sem(f"w2_hi{i}") for i in range(2)]
        w2_lo = sem("w2_lo")
        wu_hi = sem("wu_hi")
        wu_lo = sem("wu_lo")
        hid_made = sem("hid_made")
        hid_gelu = sem("hid_gelu")
        hid_split = sem("hid_split")
        y_made = sem("y_made")
        base_done = sem("base_done")
        y_biased = sem("y_biased")
        y_turned = sem("y_turned")
        y_weighted = sem("y_weighted")
        slots_turned = sem("slots_turned")
        slots_hi = sem("slots_hi")
        slots_lo = sem("slots_lo")
        slot_math = sem("slot_math")
        slots_sided = sem("slots_sided")

        x_v = x.rearrange("b c f -> (b c) f").rearrange("(t p) f -> p t f", p=P)
        out_v = out[0:T, :].rearrange("(t p) f -> p t f", p=P)
        spare_v = out[T:T + SLOTS, :].rearrange("(p j) f -> p j f", p=64)
        cond_v = cond_w.rearrange("s c d -> s (c d)")
        diag_v = cond_rows.rearrange("(t g) (c d) -> g c t d", g=SPT, c=C)
        fill_v = slot_rows.rearrange("(p j) f -> p j f", p=P)
        w1_v = w1.rearrange("e (k p) f -> e p k f", p=P)
        w2_v = w2.rearrange("e (t p) f -> e p t f", p=P)
        wd_v = wd.rearrange("e (k p) r -> e p k r", p=P)
        slots_a = slot_rows.rearrange("(e s) f -> e s f", e=E)[:, 0:2 * P, :].rearrange("e (t p) f -> e p t f", p=P)
        slots_b = slot_rows.rearrange("(e s) f -> e s f", e=E)[:, 2 * P:SLOTS, :]

        def hid_count(u, j):
            return u * HT + (j + 1)

        def hid_before(v):
            return v * HT

        def y_before(v):
            return 2 * HTILES + (v - 2) * KD

        block = ctx.enter_context(nc.Block())

        @block.sync
        def _(sp):
            def load_first(v):
                e = v - 1
                sp.wait_ge(w1_lo, v * CHUNKS)
                sp.dma_start(w1_raw[:, :, :], w1_v[e]).then_inc(w1_in, 16)
                sp.wait_ge(wd_lo, v)
                sp.dma_start(wd_raw[:, :, :], wd_v[e]).then_inc(wd_in, 16)
                sp.wait_ge(wu_lo, v)
                for g in range(3):
                    sp.dma_start(wu_raw[g * RANK:(g + 1) * RANK, :], wu[e]).then_inc(wu_in, 16)

            def load_second(v):
                sp.wait_ge(w2_lo, v * CHUNKS)
                sp.dma_start(w2_raw[:, :, :], w2_v[v - 1]).then_inc(w2_in, 16)

            def load_slots(e, par, first=False):
                if not first:
                    sp.wait_ge(slots_turned, (e - 1) * KD)
                    sp.wait_ge(slots_sided, (e - 1) * KD)
                sp.dma_start(slot_in[par][:, 0:2, :], slots_a[e]).then_inc(slots_in[par], 16)
                sp.dma_start(slot_in[par][0:ST_ROWS[2], 2, :], slots_b[e]).then_inc(slots_in[par], 16)

            sp.dma_start(itok_col[:, :], itok.rearrange("(b a) -> b a", a=1)).then_inc(itok_in, 16)
            sp.dma_start(x_in[:, 0:HTILES, :], x_v[:, 0:HTILES, :]).then_inc(x_loaded[0], 16)
            sp.wait_ge(cond_in, 16)
            sp.dma_start(cond_rows, cond_g[:, :]).then_inc(cond_out, 16)
            sp.dma_start(x_in[:, HTILES:NT, :], x_v[:, HTILES:NT, :]).then_inc(x_loaded[1], 16)
            sp.wait_ge(cond_out, 16)
            sp.wait_ge(diag_zero, 1)
            for g in range(SPT):
                rows = slice(g * C, (g + 1) * C)
                sp.dma_start(cond_diag[rows, :, rows], diag_v[g]).then_inc(diag_in, 16)
            sp.dma_start(w1_raw[:, :, :], sw1.rearrange("(k p) f -> p k f", p=P)).then_inc(w1_in, 16)
            sp.dma_start(wd_raw[:, :, :], swd.rearrange("(k p) r -> p k r", p=P)).then_inc(wd_in, 16)
            sp.dma_start(w2_raw[:, :, :], sw2.rearrange("(t p) f -> p t f", p=P)).then_inc(w2_in, 16)
            for g in range(3):
                sp.dma_start(wu_raw[g * RANK:(g + 1) * RANK, :], swu).then_inc(wu_in, 16)
            sp.wait_ge(empty_made, 2)
            sp.dma_start(fill_v, empty_row[:, :].unsqueeze(1).to_broadcast([P, E * SLOTS // P, ROW])).then_inc(filled, 16)
            sp.dma_start(spare_v, empty_row[0:64, 0:D].unsqueeze(1).to_broadcast([64, SLOTS // 64, D])).then_inc(spare_out, 16)
            load_first(1)
            load_second(1)
            sp.wait_ge(dispatched, 16 * NT * K)
            sp.wait_ge(consts, 11)
            load_slots(0, 0, first=True)
            load_slots(1, 1, first=True)
            for h in range(2):
                sp.wait_ge(base_done, (h + 1) * HTILES)
                sp.dma_start(out_v[:, h * HTILES:(h + 1) * HTILES, :],
                             base[:, h * HTILES:(h + 1) * HTILES, :]).then_inc(base_out, 16)
                if h == 0:
                    load_first(2)
                    load_second(2)
            with sp.Fori(0, (E - 2) // 2) as pair:
                for d in range(2):
                    load_first(pair * 2 + (3 + d))
                    load_slots(pair * 2 + (2 + d), d % 2)
                    load_second(pair * 2 + (3 + d))
            sp.wait_ge(filled, 16)
            sp.wait_ge(spare_out, 16)
            sp.wait_ge(base_out, 32)
            sp.wait_ge(dispatched, 16 * NT * K)
            sp.wait_ge(combined, 16 * ST * E)

        @block.gpsimd
        def _(pool):
            pool.memset(ident[:, :], 0.0).then_inc(ident_made, 1)
            pool.wait_ge(ident_made, 1)
            pool.affine_select(out=ident[:, :], in_=ident[:, :], compare_op=ALU.not_equal, fill=1.0, base=0,
                               pattern=[[-1, P]], channel_multiplier=1).then_inc(ident_made, 1)
            pool.memset(ones[:, :], 1.0).then_inc(consts, 1)
            pool.wait_ge(itok_in, 16)
            pool.indirect_dma_start(
                out=cond_g[:, :], out_offset=None, in_=cond_v,
                in_offset=bass.IndirectOffsetOnAxis(ap=itok_col[:, 0:1].bitcast(U32), axis=0)).then_inc(cond_in, 16)
            pool.memset(empty_row[:, :], 0.0).then_inc(empty_made, 1)
            pool.wait_ge(empty_made, 1)
            pool.memset(empty_row[:, ID_COL:ID_COL + 1], float(T)).then_inc(empty_made, 1)
            pool.iota(rank_of[:, :, :], pattern=[[0, NT], [-1, E]], base=E, channel_multiplier=0,
                      allow_small_or_imprecise_dtypes=True).then_inc(consts, 1)
            pool.wait_ge(consts, 2)
            pool.affine_select(out=before[:, :], in_=ones[:, :], compare_op=ALU.is_gt, fill=0.0, base=0,
                               pattern=[[1, P]], channel_multiplier=-1).then_inc(consts, 1)
            pool.iota(slot_base[:, :, :, :], pattern=[[0, NT], [CAP, K], [SLOTS, E]], base=0, channel_multiplier=0,
                      allow_small_or_imprecise_dtypes=True).then_inc(consts, 1)
            pool.iota(slot_local[:, :], pattern=[[P, ST]], base=0, channel_multiplier=1,
                      allow_small_or_imprecise_dtypes=True).then_inc(consts, 1)
            for k in range(K):
                pool.iota(token_row[k][:, :, ID_COL], pattern=[[P, NT]], base=0, channel_multiplier=1,
                          allow_small_or_imprecise_dtypes=True).then_inc(consts, 1)
                pool.memset(token_row[k][:, :, ID_COL + 1:ROW], 0.0).then_inc(consts, 1)
            for i in range(2):
                pool.memset(slot_in[i][:, ST - 1, D:ROW], 0.0).then_inc(consts, 1)

            def apart(semaphore, count):
                if not isinstance(count, int):
                    count = pool.to_reg(count)
                    pool.wait_ge(ident_made, 2)
                pool.wait_ge(semaphore, count)

            def small_hi(v, par, waits=True):
                if waits:
                    pool.wait_ge(hid_made, hid_before(v))
                apart(wd_in, 16 * (v + 1))
                for g in range(3):
                    ins = pool.tensor_copy(wd_h[par][:, :, g, :], wd_raw[:, :, :])
                ins.then_inc(wd_hi, 1)
                if waits:
                    pool.wait_ge(y_made, y_before(v))
                apart(wu_in, 48 * (v + 1))
                pool.tensor_copy(wu_s[par][:, :], wu_raw[:, :]).then_inc(wu_hi, 1)

            def w2_hi_part(v, par):
                apart(w2_in, 16 * (v + 1))
                for c in range(ACT_W2, CHUNKS):
                    pool.tensor_copy(w2_h[par][:, c * FT:(c + 1) * FT, :],
                                     w2_raw[:, c * FT:(c + 1) * FT, :]).then_inc(w2_hi[1], 1)

            def set_bias(e, par):
                pool.tensor_copy(bias_now[par][:, 0:NF], bias_t[:, bass.ds(e * NF, NF)]).then_inc(bias_set, 1)
                pool.tensor_copy(bias_now[par][:, NF:NF + KD],
                                 bias_t[:, bass.ds(e * KD + (N_BIAS1 + N_SBIAS1), KD)]).then_inc(bias_set, 1)

            def side_data(e, par):
                apart(slots_in[par], (e + (2 - par)) * 16)
                pool.tensor_copy(slot_w[par][:, :], slot_in[par][:, :, W_COL]).then_inc(slot_math, 1)
                pool.tensor_scalar(slot_free[:, :], slot_in[par][:, :, ID_COL], float(T), None,
                                   ALU.is_ge).then_inc(slot_math, 1)
                pool.wait_ge(slot_math, e * SIDE + 2)
                pool.tensor_tensor(slot_spare[:, :], slot_free[:, :], slot_local[:, :], ALU.mult).then_inc(slot_math, 1)
                pool.wait_ge(slot_math, e * SIDE + 3)
                pool.tensor_tensor(slot_row[:, :], slot_spare[:, :], slot_in[par][:, :, ID_COL],
                                   ALU.add).then_inc(slot_math, 1)
                apart(slot_math, e * SIDE + 4)
                pool.tensor_copy(slot_tok[par][:, :], slot_row[:, :]).then_inc(slots_sided, KD)

            def combine(e, par):
                pool.wait_ge(y_weighted, (e + 1) * ST)
                apart(slots_sided, (e + 1) * KD)
                if not isinstance(e, int) or e > 0:
                    apart(combined, e * (16 * ST))
                for s in range(ST):
                    n = ST_ROWS[s]
                    pool.indirect_dma_start(
                        out=out, out_offset=bass.IndirectOffsetOnAxis(ap=slot_tok[par][0:n, s:s + 1].bitcast(U32), axis=0),
                        in_=y_row[0:n, s, :], in_offset=None, bounds_check=T + SLOTS - 1,
                        compute_op=ALU.add).then_inc(combined, 16)

            small_hi(0, 0, waits=False)
            for c in range(CHUNKS):
                pool.wait_ge(w2_hi[0], c + 1)
                rows = slice(c * FT, (c + 1) * FT)
                pool.tensor_tensor(w2_l[0][:, rows, :], w2_raw[:, rows, :], w2_h[0][:, rows, :].bitcast(F32),
                                   ALU.subtract).then_inc(w2_lo, 1)
            for b in range(NT // 2):
                pool.wait_ge(rows_copied, b + 1)
                pool.tensor_copy(token_row[1][:, 2 * b:2 * b + 2, 0:D],
                                 token_row[0][:, 2 * b:2 * b + 2, 0:D]).then_inc(rows_twice, 1)
            pool.wait_ge(bias_ready, 1)
            set_bias(0, 0)
            small_hi(1, 1, waits=False)
            pool.wait_ge(rows_copied, NT // 2)
            pool.wait_ge(rows_twice, NT // 2)
            pool.wait_ge(slots_known, 3)
            pool.wait_ge(filled, 16)
            for t in range(NT):
                for k in range(K):
                    pool.indirect_dma_start(
                        out=slot_rows, out_offset=bass.IndirectOffsetOnAxis(ap=slot_i[:, t, k:k + 1].bitcast(U32), axis=0),
                        in_=token_row[k][:, t, :], in_offset=None, bounds_check=E * SLOTS - 1,
                        oob_is_err=False).then_inc(dispatched, 16)

            def period(e, par, combine_one=True, split=True, biases=True):
                if split:
                    small_hi(e + 2, par)
                if combine_one:
                    combine(e - 1, 1 - par)
                side_data(e, par)
                if biases:
                    if combine_one:
                        apart(y_biased, e * KD)
                    set_bias(e + 1, 1 - par)
                if split:
                    w2_hi_part(e + 2, par)

            period(0, 0, combine_one=False)
            pool.wait_ge(base_out, 32)
            pool.wait_ge(spare_out, 16)
            with pool.Fori(0, (E - 2) // 2) as pair:
                for d in range(2):
                    period(pair * 2 + (1 + d), (1 + d) % 2)
            period(7, 1, split=False, biases=False)
            combine(7, 1)

        @block.scalar
        def _(act):
            act.dma_start(gate_raw[:, :, :], gate_w.rearrange("(k p) e -> p k e", p=P)).then_inc(gate_in, 16)
            act.dma_start(bias_rows[0:N_BIAS1, :], b1.rearrange("e (t p) -> (e t) p", p=P)).then_inc(biases_in, 16)
            act.dma_start(bias_rows[N_BIAS1:N_BIAS1 + N_SBIAS1, :],
                          sb1.rearrange("(t p) -> t p", p=P)).then_inc(biases_in, 16)
            act.dma_start(bias_rows[N_BIAS1 + N_SBIAS1:N_BIAS, :],
                          b2.rearrange("e (t p) -> (e t) p", p=P)).then_inc(biases_in, 16)
            act.dma_start(sb2_all[:, :], sb2.partition_broadcast(P)).then_inc(sb2_in, 16)

            def w1_chunk(v, par, c):
                if c == 0:
                    act.wait_ge(w1_in, 16 * (v + 1))
                act.activation(w1_h[par][:, :, c * FC:(c + 1) * FC], w1_raw[:, :, c * FC:(c + 1) * FC],
                               ACT.Copy).then_inc(w1_hi, 1)

            def w2_chunk(v, par, c):
                if c == 0:
                    act.wait_ge(w2_in, 16 * (v + 1))
                    if not isinstance(v, int) or v >= 2:
                        act.wait_ge(y_made, y_before(v))
                act.activation(w2_h[par][:, c * FT:(c + 1) * FT, :], w2_raw[:, c * FT:(c + 1) * FT, :],
                               ACT.Copy).then_inc(w2_hi[0], 1)

            act.wait_ge(gate_in, 16)
            act.activation(gate2[:, :, 0:E], gate_raw[:, :, :], ACT.Copy).then_inc(gate_hi, 1)
            act.wait_ge(bias_turned, 1)
            act.activation(bias_t[:, :], row_ps[:, 0:N_BIAS], ACT.Copy).then_inc(bias_ready, 1)
            for h in range(2):
                for k in range(KD):
                    act.wait_ge(xct_made, h * KD + k + 1)
                    src = hid_ps[k] if h == 0 else turn_ps[k]
                    act.activation(xct_h[:, k, h * HALF:(h + 1) * HALF], src[:, :], ACT.Copy).then_inc(xct_hi, 1)
                    act.activation(xct_f[:, k, h * HALF:(h + 1) * HALF], src[:, :], ACT.Copy).then_inc(xct_kept, 1)
                    w1_chunk(0, 0, h * KD + k)
            row_banks = [y_ps[0], y_ps[1], row_ps, hid_ps[2]]
            for b in range(NT // 2):
                act.wait_ge(rows_made, b + 1)
                act.activation(token_row[0][:, 2 * b:2 * b + 2, 0:D],
                               row_banks[b][:, :].rearrange("p (t f) -> p t f", t=2), ACT.Copy).then_inc(rows_copied, 1)

            for c in range(CHUNKS):
                w2_chunk(0, 0, c)
            act.wait_ge(logits_made, 1)
            act.activation(logits2[:, :, :], turn_ps[0][:, 0:NT * 2 * E].rearrange("p (t e) -> p t e", t=NT),
                           ACT.Copy).then_inc(logits_copied, 1)
            act.wait_ge(centred, 1)
            act.activation(expd[:, :, :], logits[:, :, :], ACT.Exp).then_inc(expd_made, 1)

            def gelu_tile(u, j, n, bias):
                act.wait_ge(hid_made, hid_count(u, j))
                if isinstance(u, int) and u == 0 and j < 3:
                    pass
                else:
                    act.wait_ge(hid_split, hid_count(u, j) - 3)
                src = hid_ps[j % 3]
                if j == 0:
                    act.activation(gelu_f[2 * RANK:3 * RANK, 0, 0:n], src[2 * RANK:3 * RANK, 0:n], ACT.Gelu)
                    act.activation(low_s[:, 0:n], src[0:3 * RANK, 0:n], ACT.Gelu).then_inc(hid_gelu, 1)
                else:
                    act.activation(gelu_f[:, j % 3, 0:n], src[:, 0:n], ACT.Gelu, bias=bias(j - 1))
                    act.activation(hid_h[:, j - 1, 0:n], src[:, 0:n], ACT.Gelu, bias=bias(j - 1)).then_inc(hid_gelu, 1)

            def slots_hi_part():
                for k in range(KD):
                    act.activation(xs_h[:, k, :], turn_ps[k][:, 0:SLOTS], ACT.Copy).then_inc(slots_hi, 1)

            shared_bias = lambda f: bias_t[:, N_BIAS1 + f:N_BIAS1 + f + 1]
            for j in range(HT):
                gelu_tile(0, j, HALF, shared_bias)
            for c in range(CHUNKS):
                w1_chunk(1, 1, c)
            for c in range(CHUNKS):
                w2_chunk(1, 1, c)
            for j in range(HT):
                gelu_tile(1, j, HALF, shared_bias)
            act.wait_ge(slots_turned, KD)
            slots_hi_part()

            def period(e, par, split=True):
                act.wait_ge(bias_set, e * 2 + 2)
                for j in range(HT):
                    gelu_tile(e + 2, j, SLOTS, lambda f: bias_now[par][:, f:f + 1])
                if split:
                    for c in range(CHUNKS):
                        w1_chunk(e + 2, par, c)
                        if c == 1:
                            act.wait_ge(slots_turned, e * KD + 2 * KD)
                            slots_hi_part()
                    for c in range(ACT_W2):
                        w2_chunk(e + 2, par, c)
                for m in range(KD):
                    act.wait_ge(y_made, 2 * HTILES + (e * KD + (m + 1)))
                    act.activation(y_t[:, m, :], y_ps[m][:, 0:SLOTS], ACT.Identity,
                                   bias=bias_now[par][:, NF + m:NF + m + 1]).then_inc(y_biased, 1)

            period(0, 0)
            with act.Fori(0, (E - 2) // 2) as pair:
                for d in range(2):
                    period(pair * 2 + (1 + d), (1 + d) % 2)
            period(7, 1, split=False)

        @block.vector
        def _(dve):
            dve.memset(cond_diag[:, :, :], 0.0).then_inc(diag_zero, 1)
            dve.wait_ge(gate_in, 16)
            dve.wait_ge(gate_hi, 1)
            dve.tensor_tensor(gate2[:, :, E:2 * E], gate_raw[:, :, :], gate2[:, :, 0:E].bitcast(F32),
                              ALU.subtract).then_inc(gate_lo, 1)

            def w1_chunk(c, par, v):
                dve.wait_ge(w1_hi, v * CHUNKS + (c + 1))
                cols = slice(c * FC, (c + 1) * FC)
                dve.tensor_tensor(w1_l[par][:, :, cols], w1_raw[:, :, cols], w1_h[par][:, :, cols].bitcast(F32),
                                  ALU.subtract).then_inc(w1_lo, 1)

            def w2_chunk(c, par, v):
                if isinstance(v, int) and v == 1:
                    dve.wait_ge(w2_hi[0], CHUNKS + c + 1)
                elif c < ACT_W2:
                    dve.wait_ge(w2_hi[0], v * ACT_W2 + (2 * CHUNKS - 2 * ACT_W2 + c + 1))
                else:
                    dve.wait_ge(w2_hi[1], v * (CHUNKS - ACT_W2) + (c - ACT_W2 + 1) - 2 * (CHUNKS - ACT_W2))
                rows = slice(c * FT, (c + 1) * FT)
                dve.tensor_tensor(w2_l[par][:, rows, :], w2_raw[:, rows, :], w2_h[par][:, rows, :].bitcast(F32),
                                  ALU.subtract).then_inc(w2_lo, 1)

            def wd_part(par, v):
                dve.wait_ge(wd_hi, v + 1)
                for g in range(3):
                    ins = dve.tensor_tensor(wd_l[par][:, :, g, :], wd_raw[:, :, :], wd_h[par][:, :, g, :].bitcast(F32),
                                            ALU.subtract)
                ins.then_inc(wd_lo, 1)

            def wu_part(par, v):
                dve.wait_ge(wu_hi, v + 1)
                mid = slice(RANK, 2 * RANK)
                dve.tensor_tensor(wu_s[par][mid, :], wu_raw[mid, :], wu_s[par][mid, :].bitcast(F32),
                                  ALU.subtract).then_inc(wu_lo, 1)

            def split_tile(u, j, n):
                dve.wait_ge(hid_gelu, hid_count(u, j))
                if j == 0:
                    lo = slice(2 * RANK, 3 * RANK)
                    dve.tensor_tensor(low_s[lo, 0:n], gelu_f[lo, 0, 0:n], low_s[lo, 0:n].bitcast(F32),
                                      ALU.subtract).then_inc(hid_split, 1)
                else:
                    dve.tensor_tensor(hid_l[:, j - 1, 0:n], gelu_f[:, j % 3, 0:n], hid_h[:, j - 1, 0:n].bitcast(F32),
                                      ALU.subtract).then_inc(hid_split, 1)

            for h in range(2):
                for k in range(KD):
                    dve.wait_ge(xct_kept, h * KD + k + 1)
                    src = hid_ps[k] if h == 0 else turn_ps[k]
                    cols = slice(h * HALF, (h + 1) * HALF)
                    dve.tensor_tensor(xct_l[:, k, cols], src[:, :], xct_h[:, k, cols].bitcast(F32),
                                      ALU.subtract).then_inc(xct_lo, 1)
                    w1_chunk(h * KD + k, 0, 0)
            wd_part(0, 0)
            def fill_base():
                dve.wait_ge(sb2_in, 16)
                dve.tensor_scalar(sb2_scaled[:, :], sb2_all[:, :], SHARED_SCALE, None, ALU.mult).then_inc(sb2_made, 1)
                dve.wait_ge(sb2_made, 1)
                dve.wait_ge(rows_made, NT // 2)
                dve.tensor_tensor(base[:, :, :], x_in[:, :, :],
                                  sb2_scaled[:, :].unsqueeze(1).to_broadcast([P, NT, D]), ALU.add).then_inc(base_made, 1)

            steps = [0]

            def step(ins):
                steps[0] += 1
                ins.then_inc(route, 1)
                dve.wait_ge(route, steps[0])

            def over_e(ap):
                return ap.unsqueeze(2).to_broadcast([P, NT, E])

            dve.wait_ge(logits_copied, 1)
            step(dve.tensor_tensor(logits[:, :, :], logits2[:, :, 0:E], logits2[:, :, E:2 * E], ALU.add))
            step(dve.tensor_reduce(top[:, :], logits[:, :, :], AX_X, ALU.max))
            dve.tensor_tensor(logits[:, :, :], logits[:, :, :], over_e(top[:, :]), ALU.subtract).then_inc(centred, 1)
            wu_part(0, 0)

            def choose(k):
                if k == 0:
                    dve.wait_ge(expd_made, 1)
                    step(dve.tensor_reduce(denom[:, :], expd[:, :, :], AX_X, ALU.add))
                    step(dve.reciprocal(denom[:, :], denom[:, :]))
                    dve.wait_ge(consts, 11)
                else:
                    step(dve.scalar_tensor_tensor(out=expd[:, :, :], in0=chosen[:, :, 0, :], scalar=-4.0,
                                                  in1=expd[:, :, :], op0=ALU.mult, op1=ALU.add))
                step(dve.tensor_reduce(top[:, :], expd[:, :, :], AX_X, ALU.max))
                step(dve.tensor_tensor(is_top[:, :, :], expd[:, :, :], over_e(top[:, :]), ALU.is_equal))
                step(dve.tensor_tensor(is_top[:, :, :], is_top[:, :, :], rank_of[:, :, :], ALU.mult))
                step(dve.tensor_reduce(best[:, :], is_top[:, :, :], AX_X, ALU.max))
                step(dve.tensor_tensor(chosen[:, :, k, :], rank_of[:, :, :], over_e(best[:, :]), ALU.is_equal))
                step(dve.tensor_tensor(token_row[k][:, :, W_COL], top[:, :], denom[:, :], ALU.mult))

            def first_slots():
                dve.engine_nop().then_inc(chosen_made, 1)
                step(dve.tensor_tensor(picked[:, :, :, :], chosen[:, :, :, :], slot_base[:, :, :, :], ALU.mult))
                step(dve.tensor_reduce(base_of[:, :, :], picked[:, :, :, :], AX_X, ALU.add))

            def place_tokens():
                dve.wait_ge(pos_made, 1)
                step(dve.tensor_tensor(picked[:, :, :, :],
                                       turn_ps[0][:, 0:NT * K * E].rearrange("p (t k e) -> p t k e", t=NT, k=K),
                                       chosen[:, :, :, :], ALU.mult))
                step(dve.tensor_reduce(pos[:, :, :], picked[:, :, :, :], AX_X, ALU.add))
                dve.tensor_scalar(slot_f[:, :, :], pos[:, :, :], float(CAP), PAST_END, ALU.is_ge,
                                  ALU.mult).then_inc(slots_known, 1)
                step(dve.tensor_tensor(base_of[:, :, :], base_of[:, :, :], pos[:, :, :], ALU.add))
                dve.wait_ge(slots_known, 1)
                dve.tensor_tensor(slot_i[:, :, :], base_of[:, :, :], slot_f[:, :, :], ALU.add).then_inc(slots_known, 2)

            def shared_row(t):
                dve.wait_ge(y_made, t + 1)
                dve.scalar_tensor_tensor(out=base[:, t, :], in0=y_ps[t % 2][:, 0:D], scalar=SHARED_SCALE,
                                         in1=base[:, t, :], op0=ALU.mult, op1=ALU.add).then_inc(base_done, 1)

            def slots_lo_part(e):
                for k in range(KD):
                    dve.wait_ge(slots_hi, e * KD + (k + 1))
                    dve.tensor_tensor(xs_l[:, k, :], turn_ps[k][:, 0:SLOTS], xs_h[:, k, :].bitcast(F32),
                                      ALU.subtract).then_inc(slots_lo, 1)

            def weigh_rows(e, par):
                if not isinstance(e, int) or e > 0:
                    dve.wait_ge(combined, e * (16 * ST))
                dve.wait_ge(slot_math, e * SIDE + 1)
                for s in range(ST):
                    n = ST_ROWS[s]
                    dve.wait_ge(y_turned, e * ST + max(2, s + 1))
                    src = row_ps[0:n, s * D:(s + 1) * D] if s < 2 else y_ps[0][0:n, 0:D]
                    dve.tensor_scalar(y_row[0:n, s, :], src, slot_w[par][0:n, s:s + 1], None,
                                      ALU.mult).then_inc(y_weighted, 1)

            for j in range(HT):
                split_tile(0, j, HALF)
                if j == 0:
                    choose(0)
                if j == 2:
                    choose(1)
                if j == 3:
                    first_slots()
                if j == HT - 2:
                    place_tokens()
            fill_base()
            dve.wait_ge(base_made, 1)
            for t in range(HTILES):
                w1_chunk(t, 1, 1)
                shared_row(t)
            wd_part(1, 1)
            wu_part(1, 1)
            for j in range(HT):
                split_tile(1, j, HALF)
                if 1 <= j <= CHUNKS:
                    w2_chunk(j - 1, 1, 1)
            slots_lo_part(0)
            for t in range(HTILES, NT):
                shared_row(t)

            def period(e, par, rows=True, split=True):
                for j in range(HT):
                    split_tile(e + 2, j, SLOTS)
                    if rows and CHUNKS // 2 <= j < CHUNKS:
                        w2_chunk(j, 1 - par, e + 1)
                    if rows and j == 4:
                        weigh_rows(e - 1, 1 - par)
                if split:
                    for c in range(CHUNKS):
                        w1_chunk(c, par, e + 2)
                        if c == 1:
                            wd_part(par, e + 2)
                            wu_part(par, e + 2)
                            slots_lo_part(e + 1)
                    for c in range(CHUNKS // 2):
                        w2_chunk(c, par, e + 2)

            period(0, 0, rows=False)
            with dve.Fori(0, (E - 2) // 2) as pair:
                for d in range(2):
                    period(pair * 2 + (1 + d), (1 + d) % 2)
            period(7, 1, split=False)
            weigh_rows(7, 1)

        @block.tensor
        def _(pe):
            def three(out_ap, l_h, l_l, r_h, r_l, start, stop):
                pe.matmul(out_ap, l_h, r_h, start=start, stop=False)
                pe.matmul(out_ap, l_h, r_l, start=False, stop=False)
                return pe.matmul(out_ap, l_l, r_h, start=False, stop=stop)

            pe.wait_ge(consts, 1)
            with pe.Fori(0, WARM_UP) as _:
                for _ in range(16):
                    pe.matmul(y_ps[0][:, 0:P], ones[:, :], ones[:, :], start=True, stop=True)
            pe.wait_ge(ident_made, 2)
            pe.wait_ge(biases_in, 48)
            pe.transpose(row_ps[:, 0:N_BIAS], bias_rows[0:N_BIAS, :], ident[0:N_BIAS, 0:N_BIAS]).then_inc(bias_turned, 1)
            for h in range(2):
                pe.wait_ge(diag_in, 16 * SPT)
                pe.wait_ge(x_loaded[h], 16)
                for k in range(KD):
                    dst = hid_ps[k] if h == 0 else turn_ps[k]
                    for t in range(HTILES):
                        ins = pe.matmul(dst[:, t * P:(t + 1) * P], x_in[:, h * HTILES + t, k * P:(k + 1) * P],
                                        cond_diag[:, h * HTILES + t, :], start=True, stop=True)
                    ins.then_inc(xct_made, 1)
            pe.wait_ge(bias_ready, 1)
            row_banks = [y_ps[0], y_ps[1], row_ps, hid_ps[2]]
            for b in range(NT // 2):
                pe.wait_ge(xct_kept, (b // 2 + 1) * KD)
                for t in (2 * b, 2 * b + 1):
                    for k in range(KD):
                        ins = pe.transpose(row_banks[b][:, (t % 2) * D + k * P:(t % 2) * D + (k + 1) * P],
                                           xct_f[:, k, t * P:(t + 1) * P], ident[:, :])
                ins.then_inc(rows_made, 1)

            def gate_tokens():
                pe.wait_ge(gate_lo, 1)
                pe.wait_ge(xct_lo, 2 * KD)
                for t in range(NT):
                    cols = slice(t * P, (t + 1) * P)
                    for k in range(KD):
                        dst = turn_ps[0][:, t * 2 * E:(t + 1) * 2 * E]
                        pe.matmul(dst, xct_h[:, k, cols], gate2[:, k, :], start=(k == 0), stop=False)
                        ins = pe.matmul(dst, xct_l[:, k, cols], gate2[:, k, :], start=False, stop=(k == KD - 1))
                ins.then_inc(logits_made, 1)

            def count_before():
                pe.wait_ge(chosen_made, 1)
                flat = chosen[:, :, :, :].rearrange("p t k e -> p (t k e)")
                w = K * E
                for s in range(NT - 1, 0, -1):
                    pe.matmul(turn_ps[0][:, s * w:NT * w], ones[:, :], flat[:, 0:(NT - s) * w], start=(s == NT - 1),
                              stop=False, skip_group_check=True)
                ins = pe.matmul(turn_ps[0][:, 0:NT * w], before[:, :], flat, start=False, stop=True,
                                skip_group_check=True)
                ins.then_inc(pos_made, 1)

            def hidden(u, j, par, v, x_h, x_l, cols, n):
                if j > 0 and (j - 1) % FT == 0:
                    pe.wait_ge(w1_lo, v * CHUNKS + ((j - 1) // FT + 1))
                if j == 0:
                    pe.wait_ge(wd_lo, v + 1)
                if not isinstance(u, int) or u > 0 or j >= 3:
                    pe.wait_ge(hid_gelu, hid_count(u, j) - 3)
                m = 3 * RANK if j == 0 else P
                dst = hid_ps[j % 3][0:m, 0:n]
                for k in range(KD):
                    if j == 0:
                        l_h, l_l = (w[:, k, :, :].rearrange("p g r -> p (g r)") for w in (wd_h[par], wd_l[par]))
                    else:
                        l_h, l_l = (w[:, k, (j - 1) * P:j * P] for w in (w1_h[par], w1_l[par]))
                    ins = three(dst, l_h, l_l, x_h[:, k, cols], x_l[:, k, cols], k == 0, k == KD - 1)
                ins.then_inc(hid_made, 1)

            def shared_out(h, t):
                n = h * HTILES + t
                if t == 0:
                    pe.wait_ge(w2_lo, CHUNKS)
                    pe.wait_ge(wu_lo, 1)
                    pe.wait_ge(hid_split, h * HT + 1)
                if n >= 2:
                    pe.wait_ge(base_done, n - 1)
                else:
                    pe.wait_ge(rows_copied, NT // 2)
                dst = y_ps[n % 2][:, 0:D]
                cols = slice(t * P, (t + 1) * P)
                pe.matmul(dst, low_s[:, cols], wu_s[0][:, :], start=True, stop=False)
                for f in range(NF):
                    if t == 0:
                        pe.wait_ge(hid_split, h * HT + (f + 2))
                    ins = three(dst, hid_h[:, f, cols], hid_l[:, f, cols], w2_h[0][:, f, :], w2_l[0][:, f, :],
                                False, f == NF - 1)
                ins.then_inc(y_made, 1)

            def expert_out(e, m, par):
                v = e + 1
                if m == 0:
                    pe.wait_ge(w2_lo, v * CHUNKS + CHUNKS)
                    pe.wait_ge(wu_lo, v + 1)
                    if isinstance(e, int) and e == 0:
                        pe.wait_ge(base_done, 2 * HTILES)
                    else:
                        pe.wait_ge(y_weighted, e * ST)
                dst = y_ps[m][:, 0:SLOTS]
                cols = slice(m * P, (m + 1) * P)
                pe.wait_ge(hid_split, hid_count(e + 2, 0))
                pe.matmul(dst, wu_s[par][:, cols], low_s[:, 0:SLOTS], start=True, stop=False)
                for f in range(NF):
                    if m == 0:
                        pe.wait_ge(hid_split, hid_count(e + 2, f + 1))
                    ins = three(dst, w2_h[par][:, f, cols], w2_l[par][:, f, cols], hid_h[:, f, 0:SLOTS],
                                hid_l[:, f, 0:SLOTS], False, f == NF - 1)
                ins.then_inc(y_made, 1)

            def turn_slots(e, par):
                pe.wait_ge(slots_in[par], (e + (2 - par)) * 16)
                if isinstance(e, int) and e == 0:
                    pe.wait_ge(slots_known, 3)
                else:
                    pe.wait_ge(slots_lo, e * KD)
                for k in range(KD):
                    for s in range(ST):
                        n = ST_ROWS[s]
                        ins = pe.transpose(turn_ps[k][:, s * P:s * P + n], slot_in[par][0:n, s, k * P:(k + 1) * P],
                                           ident[0:n, 0:n])
                    ins.then_inc(slots_turned, 1)

            def turn_results(e):
                pe.wait_ge(y_biased, e * KD + KD)
                if not isinstance(e, int) or e > 0:
                    pe.wait_ge(y_weighted, e * ST)
                for s in range(ST):
                    n = ST_ROWS[s]
                    for m in range(KD):
                        dst = (row_ps[0:n, s * D + m * P:s * D + (m + 1) * P] if s < 2
                               else y_ps[0][0:n, m * P:(m + 1) * P])
                        ins = pe.transpose(dst, y_t[:, m, s * P:s * P + n], ident[:, :])
                    ins.then_inc(y_turned, 1)

            for h in range(2):
                cols = slice(h * HALF, (h + 1) * HALF)
                for j in range(HT):
                    if h == 0 and j == 0:
                        gate_tokens()
                    if h == 0 and j == 2:
                        pe.wait_ge(rows_copied, NT // 2)
                    hidden(h, j, 0, 0, xct_h, xct_l, cols, HALF)
                    if h == 0 and j == HT - 1:
                        count_before()
                if h == 1:
                    turn_slots(0, 0)
                for t in range(HTILES):
                    shared_out(h, t)

            def period(e, par, rows=True, nxt=True):
                other = 1 - par
                pe.wait_ge(slots_lo, (e + 1) * KD)
                for j in range(HT):
                    hidden(e + 2, j, other, e + 1, xs_h, xs_l, slice(0, SLOTS), SLOTS)
                    if rows and j == 2:
                        turn_results(e - 1)
                if nxt:
                    turn_slots(e + 1, other)
                for m in range(KD):
                    expert_out(e, m, other)

            period(0, 0, rows=False)
            with pe.Fori(0, (E - 2) // 2) as pair:
                for d in range(2):
                    period(pair * 2 + (1 + d), (1 + d) % 2)
            period(7, 1, nxt=False)
            turn_results(7)


_INS = ["x", "itok_B_1_198", "L0_cond_weights", "L0_ffn_gate_w", "L0_ffn_w1", "L0_ffn_b1", "L0_ffn_w2", "L0_ffn_b2",
        "L0_ffn_wd", "L0_ffn_wu", "L0_ffn_sw1", "L0_ffn_sb1", "L0_ffn_sw2", "L0_ffn_sb2", "L0_ffn_swd", "L0_ffn_swu"]


def kernel(**inputs):
    import numpy as np
    import concourse.bacc as bacc
    from concourse.bass_utils import run_bass_kernel_spmd

    nc = bacc.Bacc("TRN2", target_bir_lowering=False, num_devices=1)
    arrays, args = {}, []
    for name in _INS:
        a = np.ascontiguousarray(inputs[name])
        arrays[f"in_{name}"] = a
        args.append(nc.dram_tensor(f"in_{name}", a.shape, mybir.dt.from_np(a.dtype), kind="ExternalInput").ap())
    out = nc.dram_tensor("out_rows", (T + SLOTS, D), F32, kind="ExternalOutput").ap()
    slot_rows = nc.dram_tensor("slot_rows", (E * SLOTS, ROW), F32, kind="Internal").ap()
    cond_rows = nc.dram_tensor("cond_rows", (B, C * C), F32, kind="Internal").ap()
    build(nc, *args, out, slot_rows, cond_rows)
    r = run_bass_kernel_spmd(nc, [arrays], core_ids=[0])
    return r.results[0]["out_rows"][0:T].reshape(B, C, D)
```

```python
from contextlib import ExitStack

import concourse.bass as bass
from concourse import mybir

F32 = mybir.dt.float32
F32R = mybir.dt.float32r
BF16 = mybir.dt.bfloat16
I32 = mybir.dt.int32
U32 = mybir.dt.uint32
ALU = mybir.AluOpType
ACT = mybir.ActivationFunctionType
AX_X = mybir.AxisListType.X

P = 128
B, C, D = 32, 32, 256
T = B * C
NT = T // P
SPT = P // C
E, K = 8, 2
H = 4 * D
RANK = 32
CAP = int(T * 1.25 / E)
SLOTS = K * CAP
SHARED_SCALE = 0.2
KD = D // P
NF = H // P
HT = NF + 1
HALF = T // 2
HTILES = HALF // P
ROW = D + 4
W_COL, ID_COL = D, D + 1
ST = (SLOTS + P - 1) // P
ST_ROWS = [min(P, SLOTS - s * P) for s in range(ST)]
CHUNKS = 4
ACT_W2 = 2
LATE_LO = 1
FC = H // CHUNKS
FT = NF // CHUNKS
SIZES = [2 * P, 2 * P + P // 8, 2 * P + P // 4, SLOTS]
WARM_UP = 9
SIDE = 4
PAST_END = float(1 << 20)
N_BIAS1, N_SBIAS1 = E * NF, NF
N_BIAS = N_BIAS1 + N_SBIAS1 + E * KD


def build(nc, x, itok, cond_w, gate_w, w1, b1, w2, b2, wd, wu, sw1, sb1, sw2, sb2, swd, swu, out, slot_rows, cond_rows):
    with ExitStack() as ctx:
        def sb(name, shape, dt=F32):
            return ctx.enter_context(nc.sbuf_tensor(name, shape, dt))

        def bank(name):
            return ctx.enter_context(nc.psum_tensor(name, [P, 512], F32))

        def sem(name):
            return ctx.enter_context(nc.semaphore(name))

        hid_ps = [bank(f"hid_ps{i}") for i in range(3)]
        y_ps = [bank(f"y_ps{i}") for i in range(2)]
        turn_ps = [bank(f"turn_ps{i}") for i in range(2)]
        row_ps = bank("row_ps")

        ident = sb("ident", [P, P])
        before = sb("before", [P, P], BF16)
        ones = sb("ones", [P, P], BF16)
        rank_of = sb("rank_of", [P, NT, E])
        slot_base = sb("slot_base", [P, NT, K, E])
        used = sb("used", [P, K, E])
        used_by = sb("used_by", [P, E], I32)
        slot_local = sb("slot_local", [P, ST])
        itok_col = sb("itok_col", [B, 1], I32)
        logits = sb("logits", [P, NT, E])
        expd = sb("expd", [P, NT, E])
        is_top = sb("is_top", [P, NT, E])
        best = sb("best", [P, NT])
        top = sb("top", [P, NT])
        denom = sb("denom", [P, NT])
        chosen = sb("chosen", [P, NT, K, E], BF16)
        picked = sb("picked", [P, NT, K, E])
        base_of = sb("base_of", [P, NT, K])
        pos = sb("pos", [P, NT, K])
        slot_f = sb("slot_f", [P, NT, K])
        slot_i = sb("slot_i", [P, NT, K], I32)
        gate_raw = sb("gate_raw", [P, KD, E])
        gate2 = sb("gate2", [P, KD, 2 * E], F32R)
        bias_rows = sb("bias_rows", [P, P])
        bias_t = sb("bias_t", [P, N_BIAS])
        bias_now = [sb(f"bias_now{i}", [P, NF + KD]) for i in range(2)]
        sb2_all = sb("sb2_all", [P, D])
        sb2_scaled = sb("sb2_scaled", [P, D])
        empty_row = sb("empty_row", [P, ROW])

        x_in = sb("x_in", [P, NT, D])
        cond_g = sb("cond_g", [B, C * C])
        cond_diag = sb("cond_diag", [P, NT, P])
        token_row = [sb(f"token_row{k}", [P, NT, ROW]) for k in range(K)]
        base = sb("base", [P, NT, D])
        xct_f = base[:, :, :].rearrange("p (k a) f -> p k (a f)", k=KD)
        scores = xct_f[0:2 * E, 0, :]
        xct_h = sb("xct_h", [P, KD, T], F32R)
        xct_l = sb("xct_l", [P, KD, T], F32R)
        slot_in = [sb(f"slot_in{i}", [P, ST, ROW]) for i in range(2)]
        slot_w = [sb(f"slot_w{i}", [P, ST]) for i in range(2)]
        slot_free = sb("slot_free", [P, ST])
        slot_row = sb("slot_row", [P, ST])
        slot_spare = sb("slot_spare", [P, ST])
        slot_tok = [sb(f"slot_tok{i}", [P, ST], I32) for i in range(2)]
        xs_h = sb("xs_h", [P, KD, SLOTS], F32R)
        xs_l = sb("xs_l", [P, KD, SLOTS], F32R)
        y_t = sb("y_t", [P, KD, SLOTS])
        y_row = sb("y_row", [P, ST, D])

        w1_raw = sb("w1_raw", [P, KD, H])
        wd_raw = sb("wd_raw", [P, KD, RANK])
        w2_raw = sb("w2_raw", [P, NF, D])
        wu_raw = sb("wu_raw", [3 * RANK, D])
        w1_h = [sb(f"w1_h{i}", [P, KD, H], F32R) for i in range(2)]
        w1_l = [sb(f"w1_l{i}", [P, KD, H], F32R) for i in range(2)]
        wd_h = [sb(f"wd_h{i}", [P, KD, 3, RANK], F32R) for i in range(2)]
        wd_l = [sb(f"wd_l{i}", [P, KD, 3, RANK], F32R) for i in range(2)]
        w2_h = [sb(f"w2_h{i}", [P, NF, D], F32R) for i in range(2)]
        w2_l = [sb(f"w2_l{i}", [P, NF, D], F32R) for i in range(2)]
        wu_s = [sb(f"wu_s{i}", [3 * RANK, D], F32R) for i in range(2)]
        gelu_f = sb("gelu_f", [P, 3, HALF])
        hid_h = sb("hid_h", [P, NF, HALF], F32R)
        hid_l = sb("hid_l", [P, NF, HALF], F32R)
        low_s = sb("low_s", [3 * RANK, HALF], F32R)

        itok_in = sem("itok_in")
        x_loaded = [sem(f"x_loaded{h}") for h in range(2)]
        gate_in = sem("gate_in")
        biases_in = sem("biases_in")
        sb2_in = sem("sb2_in")
        w1_in = sem("w1_in")
        wd_in = sem("wd_in")
        w2_in = sem("w2_in")
        wu_in = sem("wu_in")
        cond_in = sem("cond_in")
        cond_out = sem("cond_out")
        diag_in = sem("diag_in")
        slots_in = [sem(f"slots_in{i}") for i in range(2)]
        filled = sem("filled")
        spare_out = sem("spare_out")
        dispatched = sem("dispatched")
        base_out = sem("base_out")
        combined = sem("combined")
        consts = sem("consts")
        ident_made = sem("ident_made")
        empty_made = sem("empty_made")
        diag_zero = sem("diag_zero")
        xct_made = sem("xct_made")
        xct_hi = sem("xct_hi")
        xct_kept = sem("xct_kept")
        xct_lo = sem("xct_lo")
        rows_made = sem("rows_made")
        rows_copied = sem("rows_copied")
        rows_twice = sem("rows_twice")
        base_made = sem("base_made")
        sb2_made = sem("sb2_made")
        gate_hi = sem("gate_hi")
        gate_lo = sem("gate_lo")
        logits_made = sem("logits_made")
        scores_made = sem("scores_made")
        scores_copied = sem("scores_copied")
        bias_turned = sem("bias_turned")
        bias_ready = sem("bias_ready")
        bias_set = sem("bias_set")
        route = sem("route")
        centred = sem("centred")
        expd_made = sem("expd_made")
        chosen_made = sem("chosen_made")
        pos_made = sem("pos_made")
        slots_known = sem("slots_known")
        used_known = sem("used_known")
        w1_hi = sem("w1_hi")
        w1_lo = sem("w1_lo")
        wd_hi = sem("wd_hi")
        wd_lo = sem("wd_lo")
        last_hi = sem("last_hi")
        w2_hi = [sem(f"w2_hi{i}") for i in range(2)]
        w2_lo = sem("w2_lo")
        wu_hi = sem("wu_hi")
        wu_lo = sem("wu_lo")
        hid_made = sem("hid_made")
        hid_gelu = sem("hid_gelu")
        hid_split = sem("hid_split")
        y_made = sem("y_made")
        base_done = sem("base_done")
        y_biased = sem("y_biased")
        y_turned = sem("y_turned")
        y_weighted = sem("y_weighted")
        slots_turned = sem("slots_turned")
        slots_hi = sem("slots_hi")
        slots_lo = sem("slots_lo")
        slot_math = sem("slot_math")
        slots_sided = sem("slots_sided")

        x_v = x.rearrange("b c f -> (b c) f").rearrange("(t p) f -> p t f", p=P)
        out_v = out[0:T, :].rearrange("(t p) f -> p t f", p=P)
        spare_v = out[T:T + SLOTS, :].rearrange("(p j) f -> p j f", p=64)
        cond_v = cond_w.rearrange("s c d -> s (c d)")
        diag_v = cond_rows.rearrange("(t g) (c d) -> g c t d", g=SPT, c=C)
        fill_v = slot_rows.rearrange("(p j) f -> p j f", p=P)
        w1_v = w1.rearrange("e (k p) f -> e p k f", p=P)
        w2_v = w2.rearrange("e (t p) f -> e p t f", p=P)
        wd_v = wd.rearrange("e (k p) r -> e p k r", p=P)
        slots_a = slot_rows.rearrange("(e s) f -> e s f", e=E)[:, 0:2 * P, :].rearrange("e (t p) f -> e p t f", p=P)
        slots_b = slot_rows.rearrange("(e s) f -> e s f", e=E)[:, 2 * P:SLOTS, :]

        def hid_count(u, j):
            return u * HT + (j + 1)

        def hid_before(v):
            return v * HT

        def hid_ring(u):
            return hid_ps + [row_ps, y_ps[1], turn_ps[1]] if isinstance(u, int) and u == 0 else hid_ps

        def hid_bank(u, j):
            return hid_ring(u)[j % len(hid_ring(u))]

        def y_before(v):
            return 2 * HTILES + (v - 2) * KD

        def by_size(engine, e, work):
            tokens = engine.value_load(used_by[0:1, bass.ds(e, 1)], min_val=0, max_val=SLOTS)

            def pick(i):
                if i == len(SIZES) - 1:
                    work(SIZES[i])
                    return
                with engine.If(tokens <= SIZES[i]):
                    work(SIZES[i])
                with engine.Else():
                    pick(i + 1)

            pick(0)

        block = ctx.enter_context(nc.Block())

        @block.sync
        def _(sp):
            def load_first(v):
                e = v - 1
                sp.wait_ge(w1_lo, v * CHUNKS)
                sp.dma_start(w1_raw[:, :, :], w1_v[e]).then_inc(w1_in, 16)
                sp.wait_ge(wd_lo, v)
                sp.dma_start(wd_raw[:, :, :], wd_v[e]).then_inc(wd_in, 16)
                sp.wait_ge(wu_lo, v)
                for g in range(3):
                    sp.dma_start(wu_raw[g * RANK:(g + 1) * RANK, :], wu[e]).then_inc(wu_in, 16)

            def load_second(v):
                sp.wait_ge(w2_lo, v * CHUNKS)
                sp.dma_start(w2_raw[:, :, :], w2_v[v - 1]).then_inc(w2_in, 16)

            def load_slots(e, par, first=False):
                if not first:
                    sp.wait_ge(slots_turned, (e - 1) * KD)
                    sp.wait_ge(slots_sided, (e - 1) * KD)
                sp.dma_start(slot_in[par][:, 0:2, :], slots_a[e]).then_inc(slots_in[par], 16)
                sp.dma_start(slot_in[par][0:ST_ROWS[2], 2, :], slots_b[e]).then_inc(slots_in[par], 16)

            sp.dma_start(itok_col[:, :], itok.rearrange("(b a) -> b a", a=1)).then_inc(itok_in, 16)
            sp.dma_start(x_in[:, 0:HTILES, :], x_v[:, 0:HTILES, :]).then_inc(x_loaded[0], 16)
            sp.wait_ge(cond_in, 16)
            sp.dma_start(cond_rows, cond_g[:, :]).then_inc(cond_out, 16)
            sp.dma_start(x_in[:, HTILES:NT, :], x_v[:, HTILES:NT, :]).then_inc(x_loaded[1], 16)
            sp.wait_ge(cond_out, 16)
            sp.wait_ge(diag_zero, 1)
            for g in range(SPT):
                rows = slice(g * C, (g + 1) * C)
                sp.dma_start(cond_diag[rows, :, rows], diag_v[g]).then_inc(diag_in, 16)
            sp.dma_start(w1_raw[:, :, :], sw1.rearrange("(k p) f -> p k f", p=P)).then_inc(w1_in, 16)
            sp.dma_start(wd_raw[:, :, :], swd.rearrange("(k p) r -> p k r", p=P)).then_inc(wd_in, 16)
            sp.dma_start(w2_raw[:, :, :], sw2.rearrange("(t p) f -> p t f", p=P)).then_inc(w2_in, 16)
            for g in range(3):
                sp.dma_start(wu_raw[g * RANK:(g + 1) * RANK, :], swu).then_inc(wu_in, 16)
            sp.wait_ge(empty_made, 2)
            sp.dma_start(fill_v, empty_row[:, :].unsqueeze(1).to_broadcast([P, E * SLOTS // P, ROW])).then_inc(filled, 16)
            sp.dma_start(spare_v, empty_row[0:64, 0:D].unsqueeze(1).to_broadcast([64, SLOTS // 64, D])).then_inc(spare_out, 16)
            load_first(1)
            load_second(1)
            sp.wait_ge(dispatched, 16 * NT * K)
            sp.wait_ge(consts, 11)
            load_slots(0, 0, first=True)
            load_slots(1, 1, first=True)
            for h in range(2):
                sp.wait_ge(base_done, (h + 1) * HTILES)
                sp.dma_start(out_v[:, h * HTILES:(h + 1) * HTILES, :],
                             base[:, h * HTILES:(h + 1) * HTILES, :]).then_inc(base_out, 16)
                if h == 0:
                    load_first(2)
                    load_second(2)
            with sp.Fori(0, (E - 2) // 2) as pair:
                for d in range(2):
                    load_first(pair * 2 + (3 + d))
                    load_slots(pair * 2 + (2 + d), d % 2)
                    load_second(pair * 2 + (3 + d))
            sp.wait_ge(filled, 16)
            sp.wait_ge(spare_out, 16)
            sp.wait_ge(base_out, 32)
            sp.wait_ge(dispatched, 16 * NT * K)
            sp.wait_ge(combined, 16 * ST * E)

        @block.gpsimd
        def _(pool):
            pool.memset(ident[:, :], 0.0).then_inc(ident_made, 1)
            pool.wait_ge(ident_made, 1)
            pool.affine_select(out=ident[:, :], in_=ident[:, :], compare_op=ALU.not_equal, fill=1.0, base=0,
                               pattern=[[-1, P]], channel_multiplier=1).then_inc(ident_made, 1)
            pool.memset(ones[:, :], 1.0).then_inc(consts, 1)
            pool.wait_ge(itok_in, 16)
            pool.indirect_dma_start(
                out=cond_g[:, :], out_offset=None, in_=cond_v,
                in_offset=bass.IndirectOffsetOnAxis(ap=itok_col[:, 0:1].bitcast(U32), axis=0)).then_inc(cond_in, 16)
            pool.memset(empty_row[:, :], 0.0).then_inc(empty_made, 1)
            pool.wait_ge(empty_made, 1)
            pool.memset(empty_row[:, ID_COL:ID_COL + 1], float(T)).then_inc(empty_made, 1)
            pool.iota(rank_of[:, :, :], pattern=[[0, NT], [-1, E]], base=E, channel_multiplier=0,
                      allow_small_or_imprecise_dtypes=True).then_inc(consts, 1)
            pool.wait_ge(consts, 2)
            pool.affine_select(out=before[:, :], in_=ones[:, :], compare_op=ALU.is_gt, fill=0.0, base=0,
                               pattern=[[1, P]], channel_multiplier=-1).then_inc(consts, 1)
            pool.iota(slot_base[:, :, :, :], pattern=[[0, NT], [0, K], [SLOTS, E]], base=0, channel_multiplier=0,
                      allow_small_or_imprecise_dtypes=True).then_inc(consts, 1)
            pool.iota(slot_local[:, :], pattern=[[P, ST]], base=0, channel_multiplier=1,
                      allow_small_or_imprecise_dtypes=True).then_inc(consts, 1)
            for k in range(K):
                pool.iota(token_row[k][:, :, ID_COL], pattern=[[P, NT]], base=0, channel_multiplier=1,
                          allow_small_or_imprecise_dtypes=True).then_inc(consts, 1)
                pool.memset(token_row[k][:, :, ID_COL + 1:ROW], 0.0).then_inc(consts, 1)
            for i in range(2):
                pool.memset(slot_in[i][:, ST - 1, D:ROW], 0.0).then_inc(consts, 1)

            def apart(semaphore, count):
                if not isinstance(count, int):
                    count = pool.to_reg(count)
                    pool.wait_ge(ident_made, 2)
                pool.wait_ge(semaphore, count)

            def small_hi(v, par, waits=True):
                if waits:
                    pool.wait_ge(hid_made, hid_before(v))
                apart(wd_in, 16 * (v + 1))
                for g in range(3):
                    ins = pool.tensor_copy(wd_h[par][:, :, g, :], wd_raw[:, :, :])
                ins.then_inc(wd_hi, 1)
                if waits:
                    pool.wait_ge(y_made, y_before(v))
                apart(wu_in, 48 * (v + 1))
                pool.tensor_copy(wu_s[par][:, :], wu_raw[:, :]).then_inc(wu_hi, 1)

            def w2_hi_part(v, par):
                apart(w2_in, 16 * (v + 1))
                for c in range(ACT_W2, CHUNKS):
                    pool.tensor_copy(w2_h[par][:, c * FT:(c + 1) * FT, :],
                                     w2_raw[:, c * FT:(c + 1) * FT, :]).then_inc(w2_hi[1], 1)

            def set_bias(e, par):
                pool.tensor_copy(bias_now[par][:, 0:NF], bias_t[:, bass.ds(e * NF, NF)]).then_inc(bias_set, 1)
                pool.tensor_copy(bias_now[par][:, NF:NF + KD],
                                 bias_t[:, bass.ds(e * KD + (N_BIAS1 + N_SBIAS1), KD)]).then_inc(bias_set, 1)

            def side_data(e, par):
                apart(slots_in[par], (e + (2 - par)) * 16)
                pool.tensor_copy(slot_w[par][:, :], slot_in[par][:, :, W_COL]).then_inc(slot_math, 1)
                pool.tensor_scalar(slot_free[:, :], slot_in[par][:, :, ID_COL], float(T), None,
                                   ALU.is_ge).then_inc(slot_math, 1)
                pool.wait_ge(slot_math, e * SIDE + 2)
                pool.tensor_tensor(slot_spare[:, :], slot_free[:, :], slot_local[:, :], ALU.mult).then_inc(slot_math, 1)
                pool.wait_ge(slot_math, e * SIDE + 3)
                pool.tensor_tensor(slot_row[:, :], slot_spare[:, :], slot_in[par][:, :, ID_COL],
                                   ALU.add).then_inc(slot_math, 1)
                apart(slot_math, e * SIDE + 4)
                pool.tensor_copy(slot_tok[par][:, :], slot_row[:, :]).then_inc(slots_sided, KD)

            def combine(e, par):
                pool.wait_ge(y_weighted, (e + 1) * ST if not isinstance(e, int) else e * ST + 1)
                apart(slots_sided, (e + 1) * KD)
                if not isinstance(e, int) or e > 0:
                    apart(combined, e * (16 * ST))
                for s in range(ST):
                    n = ST_ROWS[s]
                    if isinstance(e, int) and s > 0:
                        pool.wait_ge(y_weighted, e * ST + s + 1)
                    pool.indirect_dma_start(
                        out=out, out_offset=bass.IndirectOffsetOnAxis(ap=slot_tok[par][0:n, s:s + 1].bitcast(U32), axis=0),
                        in_=y_row[0:n, s, :], in_offset=None, bounds_check=T + SLOTS - 1,
                        compute_op=ALU.add).then_inc(combined, 16)

            small_hi(0, 0, waits=False)
            pool.wait_ge(w1_in, 16)
            pool.tensor_copy(w1_h[0][:, :, H - FC:H], w1_raw[:, :, H - FC:H]).then_inc(last_hi, 1)
            pool.wait_ge(w2_in, 16)
            last = slice(NF - FT, NF)
            pool.tensor_copy(w2_h[0][:, last, :], w2_raw[:, last, :]).then_inc(last_hi, 1)
            for c in range(CHUNKS):
                if c < CHUNKS - 1:
                    pool.wait_ge(w2_hi[0], c + 1)
                else:
                    pool.wait_ge(last_hi, 2)
                rows = slice(c * FT, (c + 1) * FT)
                pool.tensor_tensor(w2_l[0][:, rows, :], w2_raw[:, rows, :], w2_h[0][:, rows, :].bitcast(F32),
                                   ALU.subtract).then_inc(w2_lo, 1)
            for b in range(NT // 2):
                pool.wait_ge(rows_copied, b + 1)
                pool.tensor_copy(token_row[1][:, 2 * b:2 * b + 2, 0:D],
                                 token_row[0][:, 2 * b:2 * b + 2, 0:D]).then_inc(rows_twice, 1)
            pool.wait_ge(bias_ready, 1)
            set_bias(0, 0)
            small_hi(1, 1, waits=False)
            pool.wait_ge(rows_copied, NT // 2)
            pool.wait_ge(rows_twice, NT // 2)
            pool.wait_ge(slots_known, 3)
            pool.wait_ge(filled, 16)
            for t in range(NT):
                for k in range(K):
                    pool.indirect_dma_start(
                        out=slot_rows, out_offset=bass.IndirectOffsetOnAxis(ap=slot_i[:, t, k:k + 1].bitcast(U32), axis=0),
                        in_=token_row[k][:, t, :], in_offset=None, bounds_check=E * SLOTS - 1,
                        oob_is_err=False).then_inc(dispatched, 16)

            def period(e, par, combine_one=True, split=True, biases=True):
                if split:
                    small_hi(e + 2, par)
                if combine_one:
                    combine(e - 1, 1 - par)
                side_data(e, par)
                if biases:
                    if combine_one:
                        apart(y_biased, e * KD)
                    set_bias(e + 1, 1 - par)
                if split:
                    w2_hi_part(e + 2, par)

            period(0, 0, combine_one=False)
            pool.wait_ge(base_out, 32)
            pool.wait_ge(spare_out, 16)
            with pool.Fori(0, (E - 2) // 2) as pair:
                for d in range(2):
                    period(pair * 2 + (1 + d), (1 + d) % 2)
            period(7, 1, split=False, biases=False)
            combine(7, 1)

        @block.scalar
        def _(act):
            act.dma_start(gate_raw[:, :, :], gate_w.rearrange("(k p) e -> p k e", p=P)).then_inc(gate_in, 16)
            act.dma_start(bias_rows[0:N_BIAS1, :], b1.rearrange("e (t p) -> (e t) p", p=P)).then_inc(biases_in, 16)
            act.dma_start(bias_rows[N_BIAS1:N_BIAS1 + N_SBIAS1, :],
                          sb1.rearrange("(t p) -> t p", p=P)).then_inc(biases_in, 16)
            act.dma_start(bias_rows[N_BIAS1 + N_SBIAS1:N_BIAS, :],
                          b2.rearrange("e (t p) -> (e t) p", p=P)).then_inc(biases_in, 16)
            act.dma_start(sb2_all[:, :], sb2.partition_broadcast(P)).then_inc(sb2_in, 16)

            def w1_chunk(v, par, c):
                if c == 0:
                    act.wait_ge(w1_in, 16 * (v + 1))
                act.activation(w1_h[par][:, :, c * FC:(c + 1) * FC], w1_raw[:, :, c * FC:(c + 1) * FC],
                               ACT.Copy).then_inc(w1_hi, 1)

            def w2_chunk(v, par, c):
                if c == 0:
                    act.wait_ge(w2_in, 16 * (v + 1))
                    if not isinstance(v, int) or v >= 2:
                        act.wait_ge(y_made, y_before(v))
                act.activation(w2_h[par][:, c * FT:(c + 1) * FT, :], w2_raw[:, c * FT:(c + 1) * FT, :],
                               ACT.Copy).then_inc(w2_hi[0], 1)

            act.wait_ge(gate_in, 16)
            act.activation(gate2[:, :, 0:E], gate_raw[:, :, :], ACT.Copy).then_inc(gate_hi, 1)
            act.wait_ge(bias_turned, 1)
            act.activation(bias_t[:, :], row_ps[:, 0:N_BIAS], ACT.Copy).then_inc(bias_ready, 1)
            for h in range(2):
                for k in range(KD):
                    act.wait_ge(xct_made, h * KD + k + 1)
                    src = hid_ps[k] if h == 0 else turn_ps[k]
                    act.activation(xct_h[:, k, h * HALF:(h + 1) * HALF], src[:, :], ACT.Copy).then_inc(xct_hi, 1)
                    act.activation(xct_f[:, k, h * HALF:(h + 1) * HALF], src[:, :], ACT.Copy).then_inc(xct_kept, 1)
            w1_chunk(0, 0, 0)
            row_banks = [y_ps[0], y_ps[1], row_ps, hid_ps[2]]
            for b in range(NT // 2):
                act.wait_ge(rows_made, b + 1)
                act.activation(token_row[0][:, 2 * b:2 * b + 2, 0:D],
                               row_banks[b][:, :].rearrange("p (t f) -> p t f", t=2), ACT.Copy).then_inc(rows_copied, 1)
                if b == 1:
                    w1_chunk(0, 0, 1)
            w1_chunk(0, 0, 2)
            for c in range(CHUNKS - 1):
                w2_chunk(0, 0, c)
            act.wait_ge(centred, 1)
            act.activation(expd[:, :, :], logits[:, :, :], ACT.Exp).then_inc(expd_made, 1)

            def gelu_tile(u, j, n, bias):
                act.wait_ge(hid_made, hid_count(u, j))
                if isinstance(u, int) and u == 0 and j < 3:
                    pass
                else:
                    act.wait_ge(hid_split, hid_count(u, j) - 3)
                src = hid_bank(u, j)
                if j == 0:
                    act.activation(gelu_f[2 * RANK:3 * RANK, 0, 0:n], src[2 * RANK:3 * RANK, 0:n], ACT.Gelu)
                    act.activation(low_s[:, 0:n], src[0:3 * RANK, 0:n], ACT.Gelu).then_inc(hid_gelu, 1)
                else:
                    act.activation(gelu_f[:, j % 3, 0:n], src[:, 0:n], ACT.Gelu, bias=bias(j - 1))
                    act.activation(hid_h[:, j - 1, 0:n], src[:, 0:n], ACT.Gelu, bias=bias(j - 1)).then_inc(hid_gelu, 1)

            def slots_hi_part():
                for k in range(KD):
                    act.activation(xs_h[:, k, :], turn_ps[k][:, 0:SLOTS], ACT.Copy).then_inc(slots_hi, 1)

            shared_bias = lambda f: bias_t[:, N_BIAS1 + f:N_BIAS1 + f + 1]
            for j in range(HT):
                gelu_tile(0, j, HALF, shared_bias)
            for c in range(CHUNKS):
                w1_chunk(1, 1, c)
            for c in range(CHUNKS):
                w2_chunk(1, 1, c)
            for j in range(HT):
                gelu_tile(1, j, HALF, shared_bias)
            act.wait_ge(slots_turned, KD)
            slots_hi_part()

            def period(e, par, split=True):
                act.wait_ge(bias_set, e * 2 + 2)

                def work(size):
                    for j in range(HT):
                        gelu_tile(e + 2, j, size, lambda f: bias_now[par][:, f:f + 1])

                by_size(act, e, work)
                if split:
                    for c in range(CHUNKS):
                        w1_chunk(e + 2, par, c)
                        if c == 1:
                            act.wait_ge(slots_turned, e * KD + 2 * KD)
                            slots_hi_part()
                    for c in range(ACT_W2):
                        w2_chunk(e + 2, par, c)
                for m in range(KD):
                    act.wait_ge(y_made, 2 * HTILES + (e * KD + (m + 1)))
                    act.activation(y_t[:, m, :], y_ps[m][:, 0:SLOTS], ACT.Identity,
                                   bias=bias_now[par][:, NF + m:NF + m + 1]).then_inc(y_biased, 1)

            act.wait_ge(used_known, 1)
            period(0, 0)
            with act.Fori(0, (E - 2) // 2) as pair:
                for d in range(2):
                    period(pair * 2 + (1 + d), (1 + d) % 2)
            period(7, 1, split=False)

        @block.vector
        def _(dve):
            dve.memset(cond_diag[:, :, :], 0.0).then_inc(diag_zero, 1)
            dve.wait_ge(gate_in, 16)
            dve.wait_ge(gate_hi, 1)
            dve.tensor_tensor(gate2[:, :, E:2 * E], gate_raw[:, :, :], gate2[:, :, 0:E].bitcast(F32),
                              ALU.subtract).then_inc(gate_lo, 1)

            def w1_chunk(c, par, v):
                if isinstance(v, int) and v == 0 and c == CHUNKS - 1:
                    dve.wait_ge(last_hi, 1)
                else:
                    dve.wait_ge(w1_hi, v * CHUNKS + (c if not isinstance(v, int) or v > 0 else c + 1))
                cols = slice(c * FC, (c + 1) * FC)
                dve.tensor_tensor(w1_l[par][:, :, cols], w1_raw[:, :, cols], w1_h[par][:, :, cols].bitcast(F32),
                                  ALU.subtract).then_inc(w1_lo, 1)

            def w2_chunk(c, par, v):
                if isinstance(v, int) and v == 1:
                    dve.wait_ge(w2_hi[0], CHUNKS + c)
                elif c < ACT_W2:
                    dve.wait_ge(w2_hi[0], v * ACT_W2 + (2 * CHUNKS - 1 - 2 * ACT_W2 + c + 1))
                else:
                    dve.wait_ge(w2_hi[1], v * (CHUNKS - ACT_W2) + (c - ACT_W2 + 1) - 2 * (CHUNKS - ACT_W2))
                rows = slice(c * FT, (c + 1) * FT)
                dve.tensor_tensor(w2_l[par][:, rows, :], w2_raw[:, rows, :], w2_h[par][:, rows, :].bitcast(F32),
                                  ALU.subtract).then_inc(w2_lo, 1)

            def wd_part(par, v):
                dve.wait_ge(wd_hi, v + 1)
                for g in range(3):
                    ins = dve.tensor_tensor(wd_l[par][:, :, g, :], wd_raw[:, :, :], wd_h[par][:, :, g, :].bitcast(F32),
                                            ALU.subtract)
                ins.then_inc(wd_lo, 1)

            def wu_part(par, v):
                dve.wait_ge(wu_hi, v + 1)
                mid = slice(RANK, 2 * RANK)
                dve.tensor_tensor(wu_s[par][mid, :], wu_raw[mid, :], wu_s[par][mid, :].bitcast(F32),
                                  ALU.subtract).then_inc(wu_lo, 1)

            def split_tile(u, j, n):
                dve.wait_ge(hid_gelu, hid_count(u, j))
                if j == 0:
                    lo = slice(2 * RANK, 3 * RANK)
                    dve.tensor_tensor(low_s[lo, 0:n], gelu_f[lo, 0, 0:n], low_s[lo, 0:n].bitcast(F32),
                                      ALU.subtract).then_inc(hid_split, 1)
                else:
                    dve.tensor_tensor(hid_l[:, j - 1, 0:n], gelu_f[:, j % 3, 0:n], hid_h[:, j - 1, 0:n].bitcast(F32),
                                      ALU.subtract).then_inc(hid_split, 1)

            for h in range(2):
                for k in range(KD):
                    dve.wait_ge(xct_kept, h * KD + k + 1)
                    src = hid_ps[k] if h == 0 else turn_ps[k]
                    cols = slice(h * HALF, (h + 1) * HALF)
                    dve.tensor_tensor(xct_l[:, k, cols], src[:, :], xct_h[:, k, cols].bitcast(F32),
                                      ALU.subtract).then_inc(xct_lo, 1)
                if h == 0:
                    wd_part(0, 0)
            for h in range(2):
                dve.wait_ge(scores_made, h + 1)
                dve.tensor_copy(scores[:, h * HALF:(h + 1) * HALF], hid_ps[h][0:2 * E, :]).then_inc(scores_copied, 1)
                if h == 0:
                    w1_chunk(0, 0, 0)
            for c in range(1, CHUNKS):
                w1_chunk(c, 0, 0)
            def scale_sb2():
                dve.wait_ge(sb2_in, 16)
                dve.tensor_scalar(sb2_scaled[:, :], sb2_all[:, :], SHARED_SCALE, None, ALU.mult).then_inc(sb2_made, 1)
                dve.wait_ge(rows_made, NT // 2)

            def fill_base(b):
                dve.wait_ge(sb2_made, 1)
                two = slice(2 * b, 2 * b + 2)
                dve.tensor_tensor(base[:, two, :], x_in[:, two, :],
                                  sb2_scaled[:, :].unsqueeze(1).to_broadcast([P, 2, D]), ALU.add).then_inc(base_made, 1)

            steps = [0]

            def step(ins):
                steps[0] += 1
                ins.then_inc(route, 1)
                dve.wait_ge(route, steps[0])

            def over_e(ap):
                return ap.unsqueeze(2).to_broadcast([P, NT, E])

            dve.wait_ge(logits_made, 1)
            step(dve.tensor_reduce(logits[:, :, :], turn_ps[0][:, 0:NT * 2 * E].rearrange(
                "p (t part e) -> p t e part", t=NT, part=2), AX_X, ALU.add))
            step(dve.tensor_reduce(top[:, :], logits[:, :, :], AX_X, ALU.max))
            dve.tensor_tensor(logits[:, :, :], logits[:, :, :], over_e(top[:, :]), ALU.subtract).then_inc(centred, 1)
            wu_part(0, 0)

            def choose(k):
                if k == 0:
                    dve.wait_ge(expd_made, 1)
                    step(dve.tensor_reduce(denom[:, :], expd[:, :, :], AX_X, ALU.add))
                    step(dve.reciprocal(denom[:, :], denom[:, :]))
                    dve.wait_ge(consts, 11)
                else:
                    step(dve.scalar_tensor_tensor(out=expd[:, :, :], in0=chosen[:, :, 0, :], scalar=-4.0,
                                                  in1=expd[:, :, :], op0=ALU.mult, op1=ALU.add))
                step(dve.tensor_reduce(top[:, :], expd[:, :, :], AX_X, ALU.max))
                step(dve.tensor_tensor(is_top[:, :, :], expd[:, :, :], over_e(top[:, :]), ALU.is_equal))
                step(dve.tensor_tensor(is_top[:, :, :], is_top[:, :, :], rank_of[:, :, :], ALU.mult))
                step(dve.tensor_reduce(best[:, :], is_top[:, :, :], AX_X, ALU.max))
                step(dve.tensor_tensor(chosen[:, :, k, :], rank_of[:, :, :], over_e(best[:, :]), ALU.is_equal))
                step(dve.tensor_tensor(token_row[k][:, :, W_COL], top[:, :], denom[:, :], ALU.mult))

            def first_slots():
                dve.engine_nop().then_inc(chosen_made, 1)
                step(dve.tensor_tensor(picked[:, :, :, :], chosen[:, :, :, :], slot_base[:, :, :, :], ALU.mult))
                step(dve.tensor_reduce(base_of[:, :, :], picked[:, :, :, :], AX_X, ALU.add))

            def place_tokens():
                dve.wait_ge(pos_made, 1)
                step(dve.tensor_scalar(used[:, :, :], turn_ps[0][:, NT * K * E:(NT + 1) * K * E].rearrange(
                    "p (k e) -> p k e", k=K), float(CAP), None, ALU.min))
                step(dve.tensor_tensor(is_top[:, :, :], used[:, 0:1, :].to_broadcast([P, NT, E]),
                                       chosen[:, :, 1, :], ALU.mult))
                step(dve.tensor_reduce(best[:, :], is_top[:, :, :], AX_X, ALU.add))
                step(dve.tensor_tensor(base_of[:, :, 1], base_of[:, :, 1], best[:, :], ALU.add))
                step(dve.tensor_tensor(picked[:, :, :, :],
                                       turn_ps[0][:, 0:NT * K * E].rearrange("p (t k e) -> p t k e", t=NT, k=K),
                                       chosen[:, :, :, :], ALU.mult))
                step(dve.tensor_reduce(pos[:, :, :], picked[:, :, :, :], AX_X, ALU.add))
                dve.tensor_scalar(slot_f[:, :, :], pos[:, :, :], float(CAP), PAST_END, ALU.is_ge,
                                  ALU.mult).then_inc(slots_known, 1)
                step(dve.tensor_tensor(base_of[:, :, :], base_of[:, :, :], pos[:, :, :], ALU.add))
                dve.wait_ge(slots_known, 1)
                dve.tensor_tensor(slot_i[:, :, :], base_of[:, :, :], slot_f[:, :, :], ALU.add).then_inc(slots_known, 2)
                dve.tensor_tensor(used_by[:, :], used[:, 0, :], used[:, 1, :], ALU.add).then_inc(used_known, 1)

            def shared_row(t):
                dve.wait_ge(y_made, t + 1)
                dve.wait_ge(base_made, t // 2 + 1)
                dve.scalar_tensor_tensor(out=base[:, t, :], in0=y_ps[t % 2][:, 0:D], scalar=SHARED_SCALE,
                                         in1=base[:, t, :], op0=ALU.mult, op1=ALU.add).then_inc(base_done, 1)

            def slots_lo_part(e):
                for k in range(KD):
                    dve.wait_ge(slots_hi, e * KD + (k + 1))
                    dve.tensor_tensor(xs_l[:, k, :], turn_ps[k][:, 0:SLOTS], xs_h[:, k, :].bitcast(F32),
                                      ALU.subtract).then_inc(slots_lo, 1)

            def weigh_rows(e, par):
                if not isinstance(e, int) or e > 0:
                    dve.wait_ge(combined, e * (16 * ST))
                dve.wait_ge(slot_math, e * SIDE + 1)
                for s in range(ST):
                    n = ST_ROWS[s]
                    dve.wait_ge(y_turned, e * ST + (1 if s == 0 else ST))
                    src = y_ps[0][0:n, 0:D] if s == 0 else row_ps[0:n, (s - 1) * D:s * D]
                    dve.tensor_scalar(y_row[0:n, s, :], src, slot_w[par][0:n, s:s + 1], None,
                                      ALU.mult).then_inc(y_weighted, 1)

            choose(0)
            for j in range(HT):
                split_tile(0, j, HALF)
                if j == 1:
                    choose(1)
                if j == 4:
                    first_slots()
                    scale_sb2()
                if HT - 3 <= j < HT - 1:
                    fill_base(j - (HT - 3))
            place_tokens()
            for t in range(HTILES):
                shared_row(t)
                if t < 2:
                    fill_base(HTILES // 2 + t)
                w1_chunk(t, 1, 1)
            wd_part(1, 1)
            wu_part(1, 1)
            for j in range(HT):
                split_tile(1, j, HALF)
                if 1 <= j <= CHUNKS:
                    w2_chunk(j - 1, 1, 1)
            for t in range(HTILES, NT):
                shared_row(t)
                if t == HTILES + 1:
                    slots_lo_part(0)

            def period(e, par, rows=True, split=True):
                for j in range(HT):
                    split_tile(e + 2, j, SLOTS)
                    if rows and 0 <= j - 2 < LATE_LO:
                        w2_chunk(CHUNKS - LATE_LO + (j - 2), 1 - par, e + 1)
                    if rows and j == 3:
                        weigh_rows(e - 1, 1 - par)
                if split:
                    for c in range(CHUNKS):
                        w1_chunk(c, par, e + 2)
                        if c == 1:
                            wd_part(par, e + 2)
                            wu_part(par, e + 2)
                            slots_lo_part(e + 1)
                    for c in range(CHUNKS - LATE_LO):
                        w2_chunk(c, par, e + 2)

            period(0, 0, rows=False)
            with dve.Fori(0, (E - 2) // 2) as pair:
                for d in range(2):
                    period(pair * 2 + (1 + d), (1 + d) % 2)
            period(7, 1, split=False)
            weigh_rows(7, 1)

        @block.tensor
        def _(pe):
            def three(out_ap, l_h, l_l, r_h, r_l, start, stop):
                pe.matmul(out_ap, l_h, r_h, start=start, stop=False)
                pe.matmul(out_ap, l_h, r_l, start=False, stop=False)
                return pe.matmul(out_ap, l_l, r_h, start=False, stop=stop)

            pe.wait_ge(consts, 1)
            with pe.Fori(0, WARM_UP) as _:
                for _ in range(16):
                    pe.matmul(y_ps[0][:, 0:P], ones[:, :], ones[:, :], start=True, stop=True)
            pe.wait_ge(ident_made, 2)
            pe.wait_ge(biases_in, 48)
            pe.transpose(row_ps[:, 0:N_BIAS], bias_rows[0:N_BIAS, :], ident[0:N_BIAS, 0:N_BIAS]).then_inc(bias_turned, 1)
            for h in range(2):
                pe.wait_ge(diag_in, 16 * SPT)
                pe.wait_ge(x_loaded[h], 16)
                for k in range(KD):
                    dst = hid_ps[k] if h == 0 else turn_ps[k]
                    for t in range(HTILES):
                        ins = pe.matmul(dst[:, t * P:(t + 1) * P], x_in[:, h * HTILES + t, k * P:(k + 1) * P],
                                        cond_diag[:, h * HTILES + t, :], start=True, stop=True)
                    ins.then_inc(xct_made, 1)
            def turn_rows(b):
                pe.wait_ge(xct_kept, (b // 2 + 1) * KD)
                for t in (2 * b, 2 * b + 1):
                    for k in range(KD):
                        ins = pe.transpose(row_banks[b][:, (t % 2) * D + k * P:(t % 2) * D + (k + 1) * P],
                                           xct_f[:, k, t * P:(t + 1) * P], ident[:, :])
                ins.then_inc(rows_made, 1)

            def score(h):
                pe.wait_ge(gate_lo, 1)
                pe.wait_ge(xct_lo, (h + 1) * KD)
                cols = slice(h * HALF, (h + 1) * HALF)
                for k in range(KD):
                    pe.matmul(hid_ps[h][0:2 * E, :], gate2[:, k, :], xct_h[:, k, cols], start=(k == 0), stop=False)
                    ins = pe.matmul(hid_ps[h][0:2 * E, :], gate2[:, k, :], xct_l[:, k, cols], start=False,
                                    stop=(k == KD - 1))
                ins.then_inc(scores_made, 1)

            def gate_tokens():
                pe.wait_ge(scores_copied, 2)
                for t in range(NT):
                    ins = pe.transpose(turn_ps[0][:, t * 2 * E:(t + 1) * 2 * E], scores[:, t * P:(t + 1) * P],
                                       ident[0:2 * E, 0:2 * E])
                ins.then_inc(logits_made, 1)

            pe.wait_ge(bias_ready, 1)
            row_banks = [y_ps[0], y_ps[1], row_ps, hid_ps[2]]
            for h in range(2):
                turn_rows(2 * h)
                turn_rows(2 * h + 1)
                score(h)

            def count_before():
                pe.wait_ge(chosen_made, 1)
                flat = chosen[:, :, :, :].rearrange("p t k e -> p (t k e)")
                w = K * E
                for s in range(NT, 0, -1):
                    pe.matmul(turn_ps[0][:, s * w:(NT + 1) * w], ones[:, :], flat[:, 0:(NT + 1 - s) * w],
                              start=(s == NT), stop=False, skip_group_check=True)
                ins = pe.matmul(turn_ps[0][:, 0:NT * w], before[:, :], flat, start=False, stop=True,
                                skip_group_check=True)
                ins.then_inc(pos_made, 1)

            def hidden(u, j, par, v, x_h, x_l, cols, n):
                if j > 0 and (j - 1) % FT == 0:
                    pe.wait_ge(w1_lo, v * CHUNKS + ((j - 1) // FT + 1))
                if j == 0:
                    pe.wait_ge(wd_lo, v + 1)
                if not isinstance(u, int) or u > 0 or j >= len(hid_ring(0)):
                    pe.wait_ge(hid_gelu, hid_count(u, j) - len(hid_ring(u)))
                m = 3 * RANK if j == 0 else P
                dst = hid_bank(u, j)[0:m, 0:n]
                for k in range(KD):
                    if j == 0:
                        l_h, l_l = (w[:, k, :, :].rearrange("p g r -> p (g r)") for w in (wd_h[par], wd_l[par]))
                    else:
                        l_h, l_l = (w[:, k, (j - 1) * P:j * P] for w in (w1_h[par], w1_l[par]))
                    ins = three(dst, l_h, l_l, x_h[:, k, cols], x_l[:, k, cols], k == 0, k == KD - 1)
                ins.then_inc(hid_made, 1)

            def shared_out(h, t):
                n = h * HTILES + t
                if t == 0:
                    pe.wait_ge(w2_lo, CHUNKS)
                    pe.wait_ge(wu_lo, 1)
                    pe.wait_ge(hid_split, h * HT + 1)
                if n >= 2:
                    pe.wait_ge(base_done, n - 1)
                else:
                    pe.wait_ge(rows_copied, NT // 2)
                dst = y_ps[n % 2][:, 0:D]
                cols = slice(t * P, (t + 1) * P)
                pe.matmul(dst, low_s[:, cols], wu_s[0][:, :], start=True, stop=False)
                for f in range(NF):
                    if t == 0:
                        pe.wait_ge(hid_split, h * HT + (f + 2))
                    ins = three(dst, hid_h[:, f, cols], hid_l[:, f, cols], w2_h[0][:, f, :], w2_l[0][:, f, :],
                                False, f == NF - 1)
                ins.then_inc(y_made, 1)

            def expert_out(e, m, par, size):
                v = e + 1
                if m == 0:
                    pe.wait_ge(w2_lo, v * CHUNKS + CHUNKS)
                    pe.wait_ge(wu_lo, v + 1)
                    if isinstance(e, int) and e == 0:
                        pe.wait_ge(base_done, 2 * HTILES)
                    else:
                        pe.wait_ge(y_weighted, e * ST)
                dst = y_ps[m][:, 0:size]
                cols = slice(m * P, (m + 1) * P)
                pe.wait_ge(hid_split, hid_count(e + 2, 0))
                pe.matmul(dst, wu_s[par][:, cols], low_s[:, 0:size], start=True, stop=False)
                for f in range(NF):
                    if m == 0:
                        pe.wait_ge(hid_split, hid_count(e + 2, f + 1))
                    ins = three(dst, w2_h[par][:, f, cols], w2_l[par][:, f, cols], hid_h[:, f, 0:size],
                                hid_l[:, f, 0:size], False, f == NF - 1)
                ins.then_inc(y_made, 1)

            def turn_slots(e, par):
                pe.wait_ge(slots_in[par], (e + (2 - par)) * 16)
                if isinstance(e, int) and e == 0:
                    pe.wait_ge(slots_known, 3)
                else:
                    pe.wait_ge(slots_lo, e * KD)
                for k in range(KD):
                    for s in range(ST):
                        n = ST_ROWS[s]
                        ins = pe.transpose(turn_ps[k][:, s * P:s * P + n], slot_in[par][0:n, s, k * P:(k + 1) * P],
                                           ident[0:n, 0:n])
                    ins.then_inc(slots_turned, 1)

            def turn_results(e):
                pe.wait_ge(y_biased, e * KD + 1)
                if not isinstance(e, int) or e > 0:
                    pe.wait_ge(y_weighted, e * ST)
                for m in range(KD):
                    if m > 0:
                        pe.wait_ge(y_biased, e * KD + (m + 1))
                    for s in range(ST):
                        n = ST_ROWS[s]
                        dst = (y_ps[0][0:n, m * P:(m + 1) * P] if s == 0
                               else row_ps[0:n, (s - 1) * D + m * P:(s - 1) * D + (m + 1) * P])
                        ins = pe.transpose(dst, y_t[:, m, s * P:s * P + n], ident[:, :])
                        if m == KD - 1:
                            ins.then_inc(y_turned, 1)

            for h in range(2):
                cols = slice(h * HALF, (h + 1) * HALF)
                for j in range(HT):
                    if h == 0 and j < 2:
                        pe.wait_ge(scores_copied, j + 1)
                    if h == 0 and j == 2:
                        pe.wait_ge(rows_copied, NT // 2)
                    hidden(h, j, 0, 0, xct_h, xct_l, cols, HALF)
                    if h == 0 and j == 0:
                        gate_tokens()
                    if h == 0 and j == HT - 1:
                        count_before()
                for t in range(HTILES):
                    shared_out(h, t)
                    if h == 1 and t == 1:
                        turn_slots(0, 0)

            def period(e, par, rows=True, nxt=True):
                other = 1 - par

                def work(size):
                    pe.wait_ge(slots_lo, (e + 1) * KD)
                    for j in range(HT):
                        hidden(e + 2, j, other, e + 1, xs_h, xs_l, slice(0, size), size)
                        if rows and j == 2:
                            turn_results(e - 1)
                    if nxt:
                        turn_slots(e + 1, other)
                    for m in range(KD):
                        expert_out(e, m, other, size)

                by_size(pe, e, work)

            pe.wait_ge(used_known, 1)
            period(0, 0, rows=False)
            with pe.Fori(0, (E - 2) // 2) as pair:
                for d in range(2):
                    period(pair * 2 + (1 + d), (1 + d) % 2)
            period(7, 1, nxt=False)
            turn_results(7)


_INS = ["x", "itok_B_1_198", "L0_cond_weights", "L0_ffn_gate_w", "L0_ffn_w1", "L0_ffn_b1", "L0_ffn_w2", "L0_ffn_b2",
        "L0_ffn_wd", "L0_ffn_wu", "L0_ffn_sw1", "L0_ffn_sb1", "L0_ffn_sw2", "L0_ffn_sb2", "L0_ffn_swd", "L0_ffn_swu"]


def kernel(**inputs):
    import numpy as np
    import concourse.bacc as bacc
    from concourse.bass_utils import run_bass_kernel_spmd

    nc = bacc.Bacc("TRN2", target_bir_lowering=False, num_devices=1)
    arrays, args = {}, []
    for name in _INS:
        a = np.ascontiguousarray(inputs[name])
        arrays[f"in_{name}"] = a
        args.append(nc.dram_tensor(f"in_{name}", a.shape, mybir.dt.from_np(a.dtype), kind="ExternalInput").ap())
    out = nc.dram_tensor("out_rows", (T + SLOTS, D), F32, kind="ExternalOutput").ap()
    slot_rows = nc.dram_tensor("slot_rows", (E * SLOTS, ROW), F32, kind="Internal").ap()
    cond_rows = nc.dram_tensor("cond_rows", (B, C * C), F32, kind="Internal").ap()
    build(nc, *args, out, slot_rows, cond_rows)
    r = run_bass_kernel_spmd(nc, [arrays], core_ids=[0])
    return r.results[0]["out_rows"][0:T].reshape(B, C, D)
```
